# Optimizing a Trainium2 kernel written in Bass

```python
import numpy as np
import jax
import jax.numpy as jnp

def _softmax(x, axis=-1):
    return jax.nn.softmax(x, axis=axis)

def _gelu(x):
    return jax.nn.gelu(x, approximate=True)

def _silu(x):
    return jax.nn.silu(x)

def _sigmoid(x):
    return jax.nn.sigmoid(x)

def _layernorm(x, axis=-1, eps=1e-05):
    m = jnp.mean(x, axis=axis, keepdims=True)
    v = jnp.var(x, axis=axis, keepdims=True)
    return (x - m) / jnp.sqrt(v + eps)

def _scatter_add(tgt, idx, src, axis=0):
    return tgt.at[idx].add(src)

def _segment_sum(src, seg, n):
    return jax.ops.segment_sum(src, seg, n)
kernel_name = 'mk_xattn_ffn_d1_seqx_r4_b780c4'

def setup_inputs(seed: int=0):
    np.random.seed(seed)
    _w = jnp.asarray

    def _rec_inputs():
        import jax
        import jax.numpy as jnp
        _rk = jax.random.key(seed)
        x = 7.22e-05 + 1 * jax.random.normal(jax.random.fold_in(_rk, 1), (1, 2048, 256), jnp.float32)
        _lenS = 2048 - jax.random.randint(jax.random.fold_in(_rk, 7), (1,), 0, max(1, 2048 // 4) + 1, jnp.int32)
        _lenS2 = 1601 - jax.random.randint(jax.random.fold_in(_rk, 8), (1,), 0, max(1, 1601 // 4) + 1, jnp.int32)
        _ctx_1024P = jax.random.normal(jax.random.fold_in(_rk, 11), (1, 16, 256), jnp.float32)
        _ctx_1024c = jax.random.dirichlet(jax.random.fold_in(_rk, 511), 0.3 * jnp.ones((16,), jnp.float32), (1, 1601))
        _ctx_1024t = jnp.einsum('bsk,bkd->bsd', _ctx_1024c, _ctx_1024P)
        _ctx_1024t = _ctx_1024t * jax.lax.rsqrt(jnp.mean(jnp.square(_ctx_1024t)) + 1e-12) * 0.953939
        ctx_1024 = 2.81802e-05 + 1.00001 * (_ctx_1024t + 0.3 * jax.random.normal(jax.random.fold_in(_rk, 611), (1, 1601, 256), jnp.float32))
        return (x, ctx_1024)
    x, ctx_1024 = _rec_inputs()

    def _L0_xattn_setup():
        import jax, jax.numpy as jnp
        import numpy as np
        B, T, S, D = (4, 512, 1024, 256)
        TOP_K = 32

        def _read(query, mem_state, top_k, Wq, bq, Wk, bk, Wv, bv, Wo, bo):
            b, t, d = query.shape
            s = mem_state.shape[1]
            scale = 1.0 / np.sqrt(d)
            q = query @ Wq.T + bq
            k = mem_state @ Wk.T + bk
            v = mem_state @ Wv.T + bv
            scores = jnp.einsum('btd,bsd->bts', q, k) * scale
            if top_k < s:
                vals, idx = jax.lax.top_k(scores, top_k)
                b_ix = jnp.arange(b)[:, None, None]
                t_ix = jnp.arange(t)[None, :, None]
                masked = jnp.full_like(scores, -jnp.inf)
                scores = masked.at[b_ix, t_ix, idx].set(vals)
            attn = jax.nn.softmax(scores, axis=-1)
            ctx = jnp.einsum('bts,bsd->btd', attn, v)
            return ctx @ Wo.T + bo
        key = jax.random.key(seed)
        ks = jax.random.split(key, 12)
        std = 0.02
        inp = {'query': jax.random.normal(ks[0], (B, T, D), dtype=jnp.float32), 'mem_state': jax.random.normal(ks[1], (B, S, D), dtype=jnp.float32), 'top_k': TOP_K, 'Wq': jax.random.normal(ks[2], (D, D), dtype=jnp.float32) * std, 'bq': jnp.zeros((D,), dtype=jnp.float32), 'Wk': jax.random.normal(ks[3], (D, D), dtype=jnp.float32) * std, 'bk': jnp.zeros((D,), dtype=jnp.float32), 'Wv': jax.random.normal(ks[4], (D, D), dtype=jnp.float32) * std, 'bv': jnp.zeros((D,), dtype=jnp.float32), 'Wo': jax.random.normal(ks[5], (D, D), dtype=jnp.float32) * std, 'bo': jnp.zeros((D,), dtype=jnp.float32)}
        return inp
    _L0_xattn_all = _L0_xattn_setup()
    _L0_xattn_in = {k: v for k, v in _L0_xattn_all.items() if k in ('Wq', 'bq', 'Wk', 'bk', 'Wv', 'bv', 'Wo', 'bo')}
    del _L0_xattn_all

    def _L0_ffn_setup():
        import jax, jax.numpy as jnp
        import numpy as np
        EPS = 1e-05

        def rmsnorm(x):
            return x * jax.lax.rsqrt(jnp.mean(x * x, axis=-1, keepdims=True) + EPS)

        def act_quant(x):
            scale = 127.0 / jnp.clip(jnp.max(jnp.abs(x), axis=-1, keepdims=True), 1e-05)
            q = jnp.clip(jnp.round(x * scale), -128.0, 127.0) / scale
            return x + jax.lax.stop_gradient(q - x)

        def weight_quant(w):
            scale = 1.0 / jnp.clip(jnp.mean(jnp.abs(w)), 1e-05)
            q = jnp.clip(jnp.round(w * scale), -1.0, 1.0) / scale
            return w + jax.lax.stop_gradient(q - w)

        def bitlinear(x, w, b):
            xq = act_quant(rmsnorm(x))
            wq = weight_quant(w)
            return jnp.einsum('bsd,fd->bsf', xq, wq) + b
        key = jax.random.key(seed)
        k0, k1, k2 = jax.random.split(key, 3)
        B, S, D, F = (2, 2048, 256, 1024)
        x = jax.random.normal(k0, (B, S, D), dtype=jnp.float32)
        w1 = jax.random.normal(k1, (F, D), dtype=jnp.float32) * (1.0 / np.sqrt(D))
        b1 = jnp.zeros((F,), dtype=jnp.float32)
        w2 = jax.random.normal(k2, (D, F), dtype=jnp.float32) * (1.0 / np.sqrt(F))
        b2 = jnp.zeros((D,), dtype=jnp.float32)
        return {'x': x, 'w1': w1, 'b1': b1, 'w2': w2, 'b2': b2}
    _L0_ffn_all = _L0_ffn_setup()
    _L0_ffn_in = {k: v for k, v in _L0_ffn_all.items() if k in ('w1', 'b1', 'w2', 'b2')}
    del _L0_ffn_all
    return {'x': x, 'ctx_1024': ctx_1024, 'L0_xattn_Wq': _L0_xattn_in['Wq'], 'L0_xattn_bq': _L0_xattn_in['bq'], 'L0_xattn_Wk': _L0_xattn_in['Wk'], 'L0_xattn_bk': _L0_xattn_in['bk'], 'L0_xattn_Wv': _L0_xattn_in['Wv'], 'L0_xattn_bv': _L0_xattn_in['bv'], 'L0_xattn_Wo': _L0_xattn_in['Wo'], 'L0_xattn_bo': _L0_xattn_in['bo'], 'L0_ffn_w1': _L0_ffn_in['w1'], 'L0_ffn_b1': _L0_ffn_in['b1'], 'L0_ffn_w2': _L0_ffn_in['w2'], 'L0_ffn_b2': _L0_ffn_in['b2']}

def reference(x, ctx_1024, L0_xattn_Wq, L0_xattn_bq, L0_xattn_Wk, L0_xattn_bk, L0_xattn_Wv, L0_xattn_bv, L0_xattn_Wo, L0_xattn_bo, L0_ffn_w1, L0_ffn_b1, L0_ffn_w2, L0_ffn_b2):
    import jax
    import jax.numpy as jnp

    def _L0_xattn_ref(query, mem_state, top_k, Wq, bq, Wk, bk, Wv, bv, Wo, bo):
        import jax, jax.numpy as jnp
        import numpy as np
        B, T, S, D = (4, 512, 1024, 256)
        TOP_K = 32

        def _read(query, mem_state, top_k, Wq, bq, Wk, bk, Wv, bv, Wo, bo):
            b, t, d = query.shape
            s = mem_state.shape[1]
            scale = 1.0 / np.sqrt(d)
            q = query @ Wq.T + bq
            k = mem_state @ Wk.T + bk
            v = mem_state @ Wv.T + bv
            scores = jnp.einsum('btd,bsd->bts', q, k) * scale
            if top_k < s:
                vals, idx = jax.lax.top_k(scores, top_k)
                b_ix = jnp.arange(b)[:, None, None]
                t_ix = jnp.arange(t)[None, :, None]
                masked = jnp.full_like(scores, -jnp.inf)
                scores = masked.at[b_ix, t_ix, idx].set(vals)
            attn = jax.nn.softmax(scores, axis=-1)
            ctx = jnp.einsum('bts,bsd->btd', attn, v)
            return ctx @ Wo.T + bo
        return _read(query, mem_state, top_k, Wq, bq, Wk, bk, Wv, bv, Wo, bo)

    def _L0_ffn_ref(x, w1, b1, w2, b2):
        import jax, jax.numpy as jnp
        import numpy as np
        EPS = 1e-05

        def rmsnorm(x):
            return x * jax.lax.rsqrt(jnp.mean(x * x, axis=-1, keepdims=True) + EPS)

        def act_quant(x):
            scale = 127.0 / jnp.clip(jnp.max(jnp.abs(x), axis=-1, keepdims=True), 1e-05)
            q = jnp.clip(jnp.round(x * scale), -128.0, 127.0) / scale
            return x + jax.lax.stop_gradient(q - x)

        def weight_quant(w):
            scale = 1.0 / jnp.clip(jnp.mean(jnp.abs(w)), 1e-05)
            q = jnp.clip(jnp.round(w * scale), -1.0, 1.0) / scale
            return w + jax.lax.stop_gradient(q - w)

        def bitlinear(x, w, b):
            xq = act_quant(rmsnorm(x))
            wq = weight_quant(w)
            return jnp.einsum('bsd,fd->bsf', xq, wq) + b
        h = bitlinear(x, w1, b1)
        h = jax.nn.gelu(h, approximate=False)
        return bitlinear(h, w2, b2)
    x = x + _L0_xattn_ref(_layernorm(x, axis=-1), ctx_1024, 32, L0_xattn_Wq, L0_xattn_bq, L0_xattn_Wk, L0_xattn_bk, L0_xattn_Wv, L0_xattn_bv, L0_xattn_Wo, L0_xattn_bo)
    x = x + _L0_ffn_ref(_layernorm(x, axis=-1), L0_ffn_w1, L0_ffn_b1, L0_ffn_w2, L0_ffn_b2)
    return x

_drawn_inputs = setup_inputs


def setup_inputs(seed=0):
    import zlib

    import numpy as np

    out = dict(_drawn_inputs(seed))
    spreads = {'L0_xattn_bq': (0.0, 0.1),
     'L0_xattn_bk': (0.0, 0.1),
     'L0_xattn_bv': (0.0, 0.1),
     'L0_xattn_bo': (0.0, 0.1),
     'L0_ffn_b1': (0.0, 0.1),
     'L0_ffn_b2': (0.0, 0.1)}
    factors = {}
    for name, (base, spread) in spreads.items():
        noise = np.random.default_rng([zlib.crc32(name.encode()), seed]).standard_normal(out[name].shape)
        drawn = base * np.exp(spread * noise) if base else spread * noise
        out[name] = jnp.asarray(drawn.astype(out[name].dtype))
    for name, factor in factors.items():
        out[name] = (out[name] * factor).astype(out[name].dtype)
    return out
```

```python
from contextlib import ExitStack

import numpy as np

import concourse.bass as bass
from concourse import mybir

F32 = mybir.dt.float32
BF16 = mybir.dt.bfloat16
ALU = mybir.AluOpType
ACT = mybir.ActivationFunctionType
AX = mybir.AxisListType

P = 128
D = 256
DC = D // P
T = 2048
S = 1601
F = 1024
FB = F // P
BANK = 512
TOPK = 32
ROUNDS = TOPK // 8
TILES = T // P
PAIRS = TILES // 2
SB = -(-S // P)
S_LAST = S - (SB - 1) * P
SC = -(-S // BANK)
CHUNKS = [(c * BANK, min(BANK, S - c * BANK)) for c in range(SC)]
QUADS = [(g, min(g + 4, SB)) for g in range(0, SB, 4)]
NT = len(QUADS)
DV = D + 1
SCALE = float(D) ** -0.5
EPS = 1e-5
LOWEST = -3.4028234e38
MAGIC = 12582912.0
STEPS = 2 * ROUNDS

TURNS = 2 * NT + 1 + 1 + 4
RESULTS = 1 + 1 + 1 + 4 + 1
LOOP = (2, PAIRS - 1)
LAST_ROUND = PAIRS + 2


class Count:

    def __init__(self, per_round):
        self.per_round, self.before, self.loop = per_round, 0, None

    def next(self):
        n = self.before
        self.before += 1
        return n if self.loop is None else (self.loop - LOOP[0]) * self.per_round + n

    def enter(self, register):
        self.loop, self.entry = register, self.before

    def leave(self):
        assert self.before == self.entry + self.per_round
        self.loop = None
        self.before = self.entry + self.per_round * (LOOP[1] - LOOP[0])


def rounds(engine, do_round, counts=()):
    for r in range(LOOP[0]):
        do_round(r, r)
    with engine.Fori(LOOP[0], LOOP[1]) as r:
        for c in counts:
            c.enter(r)
        do_round(r, LOOP[0])
        for c in counts:
            c.leave()
    for r in range(LOOP[1], LAST_ROUND):
        do_round(r, r)


def build(nc, x, ctx, Wq, bq, Wk, bk, Wv, bv, Wo, bo, w1, b1, w2, b2, out):
    x_rows = x.rearrange("a t d -> (a t) d")
    out_rows = out.rearrange("a t d -> (a t) d")
    ctx_rows = ctx.rearrange("a s d -> (a s) d")

    with ExitStack() as stack:
        def sb(name, shape, dt=F32):
            return stack.enter_context(nc.sbuf_tensor(name, shape, dt))

        def sem(name):
            return stack.enter_context(nc.semaphore(name))

        score = [stack.enter_context(nc.psum_tensor(f"score{c}", [P, BANK], F32)) for c in range(SC)]
        turn = [stack.enter_context(nc.psum_tensor(f"turn{c}", [P, BANK], F32)) for c in range(2)]
        result = [stack.enter_context(nc.psum_tensor(f"result{c}", [P, BANK], F32)) for c in range(2)]
        prep = turn + result

        W4 = {n: sb(f"w_{n}", [P, DC, D]) for n in "qkvo"}
        WT = {n: sb(f"wt_{n}", [P, DC, D]) for n in "qkvo"}
        w1_sb = sb("w1_sb", [P, FB, D])
        w2_sb = sb("w2_sb", [P, DC, F])
        w1T = sb("w1T", [P, DC, F], BF16)
        w2T = sb("w2T", [P, FB, D], BF16)
        bq_col, bk_col, bv_col = (sb(n, [P, DC]) for n in ("bq_col", "bk_col", "bv_col"))
        bo_bc = sb("bo_bc", [P, D])
        b1_bc = sb("b1_bc", [P, F])
        b2_bc = sb("b2_bc", [P, D])
        ident = sb("ident", [P, P])
        ones = sb("ones", [P, P])
        wsum = sb("wsum", [P, 2])
        wmean = sb("wmean", [P, 2])
        winv = sb("winv", [P, 2])
        minus_half = sb("minus_half", [P, 2])
        minus_one = sb("minus_one", [P, 2])
        magic_col = sb("magic_col", [P, 1])
        unmagic_col = sb("unmagic_col", [P, 1])

        ctx_sb = sb("ctx_sb", [P, SB, D])
        ctxT = sb("ctxT", [P, DC, S])
        kT = sb("kT", [P, DC, S])
        vT = ctx_sb[:, :, :].rearrange("p b d -> p (b d)")[:, 0:DC * S].rearrange("p (c s) -> p c s", c=DC)
        vo = sb("vo", [P, SB, DV])

        x_in = sb("x_in", [P, 2, D])
        ln1_part = sb("ln1_part", [P, 2, 6])
        ln1_mv = sb("ln1_mv", [P, 2, 2])
        ln1_r = sb("ln1_r", [P, 2, 2])
        xn = sb("xn", [P, 2, D])
        xnT = sb("xnT", [P, DC, 2 * P])
        qT = sb("qT", [P, DC, 2 * P])

        s_sb = sb("s_sb", [P, 2, S])
        s_left = sb("s_left", [P, 2, S])
        best = sb("best", [P, 2, ROUNDS, 8])
        neg_max = sb("neg_max", [P, 2])
        e_all = sb("e_all", [P, 2, S])
        e_left = sb("e_left", [P, S])
        pT = sb("pT", [P, SB * P])
        inv_sum = sb("inv_sum", [P, 2])
        x_res = sb("x_res", [P, 2, D])
        x2 = sb("x2", [P, 2, D])

        ln2_part = sb("ln2_part", [P, 2, 6])
        ln2_mv = sb("ln2_mv", [P, 2, 2])
        cen = sb("cen", [P, 2, D])
        cen_max = sb("cen_max", [P, 2])
        row1 = sb("row1", [P, 12, 2])
        y1 = sb("y1", [P, 2, D])
        y1T = sb("y1T", [P, DC, 2 * P], BF16)
        g = sb("g", [P, 2, F])
        g_sq = sb("g_sq", [P, F], BF16)
        g_ssq = sb("g_ssq", [P, 2])
        g_max = sb("g_max", [P, 2])
        row2 = sb("row2", [P, 8, 2])
        y2 = sb("y2", [P, 2, F])
        y2T = sb("y2T", [P, FB, 2 * P], BF16)
        x2b = sb("x2b", [P, 2, D])
        o_sb = sb("o_sb", [P, 2, D])

        wqk_in, wvo_in, ctx_in, wff_in, bias_in = (sem(n) for n in ("wqk_in", "wvo_in", "ctx_in", "wff_in", "bias_in"))
        x_in_done, x_res_in, stored = sem("x_in_done"), sem("x_res_in"), sem("stored")
        const_ready, ident_ready = sem("const_ready"), sem("ident_ready")
        prep_ready, prep_taken = sem("prep_ready"), sem("prep_taken")
        wsum_ready, ternary_ready, wscale_step = sem("wsum_ready"), sem("ternary_ready"), sem("wscale_step")
        ln1_step, ln1_row, xn_ready, q_ready = sem("ln1_step"), sem("ln1_row"), sem("xn_ready"), sem("q_ready")
        s_ready, s_copied, topk_step, max_ready = sem("s_ready"), sem("s_copied"), sem("topk_step"), sem("max_ready")
        e_ready, e_left_ready, p_ready = sem("e_ready"), sem("e_left_ready"), sem("p_ready")
        turned, turn_taken = sem("turned"), sem("turn_taken")
        result_ready, result_taken = sem("result_ready"), sem("result_taken")
        x2_step, xb_ready = sem("x2_step"), sem("xb_ready")
        row1_step, y1_ready, x2b_ready = sem("row1_step"), sem("y1_ready"), sem("x2b_ready")
        h_ready, g_ready, g_sq_ready, g_max_ready = sem("h_ready"), sem("g_ready"), sem("g_sq_ready"), sem("g_max_ready")
        row2_step, y2_ready, o_ready = sem("row2_step"), sem("y2_ready"), sem("o_ready")

        JOB_WQK = 0
        JOB_CTX = JOB_WQK + 2
        NCTX = -(-SB // 2)
        JOB_K = JOB_CTX + NCTX
        JOB_Q0 = JOB_K + SC * DC
        JOB_WVO = JOB_Q0 + 2
        JOB_V = JOB_WVO + 2
        JOB_VO = JOB_V + SC * DC
        JOB_MEAN = JOB_VO + NCTX
        JOB_W1 = JOB_MEAN + 1
        JOB_W2 = JOB_W1 + 4
        PREPS = JOB_W2 + 4

        ROW1, ROW2, X2S = 13, 8, 7

        waits_passed = {"pool": sem("pool_waits_passed"), "dve": sem("dve_waits_passed")}

        def wait_apart(engine, semaphore, value):
            engine.wait_ge(semaphore, value)
            if not isinstance(value, int):
                engine.sem_inc(waits_passed["pool" if engine.engine == nc.gpsimd.engine else "dve"], 1)

        block = stack.enter_context(nc.Block())

        @block.sync
        def _(sp):
            def w_load(n, W, s):
                sp.dma_start(W4[n][:, :, :], W.rearrange("(c p) d -> p c d", p=P)).then_inc(s, 16)

            w_load("k", Wk, wqk_in)
            w_load("q", Wq, wqk_in)
            full = SB - 1
            half = full // 2
            sp.dma_start(ctx_sb[:, 0:half, :],
                         ctx_rows[0:half * P, :].rearrange("(b p) d -> p b d", p=P)).then_inc(ctx_in, 16)
            for u in range(2):
                sp.dma_start(x_in[:, u, :], x_rows[u * P:(u + 1) * P, :]).then_inc(x_in_done, 16)
            sp.dma_start(ctx_sb[:, half:full, :],
                         ctx_rows[half * P:full * P, :].rearrange("(b p) d -> p b d", p=P)).then_inc(ctx_in, 16)
            sp.dma_start(ctx_sb[0:S_LAST, full, :], ctx_rows[full * P:S, :]).then_inc(ctx_in, 16)
            w_load("v", Wv, wvo_in)
            w_load("o", Wo, wvo_in)
            sp.dma_start(w1_sb[:, :, :], w1.rearrange("(b p) d -> p b d", p=P)).then_inc(wff_in, 16)
            sp.dma_start(w2_sb[:, :, :], w2.rearrange("(c p) f -> p c f", p=P)).then_inc(wff_in, 16)
            for u in range(2):
                sp.dma_start(x_res[:, u, :], x_rows[u * P:(u + 1) * P, :]).then_inc(x_res_in, 16)

            def do_round(r, stage):
                if stage + 1 < PAIRS:
                    for u in range(2):
                        sp.wait_ge(xn_ready, r * 2 + u + 1)
                        sp.dma_start(x_in[:, u, :], x_rows[bass.ds((r * 2 + 2 + u) * P, P), :]).then_inc(x_in_done, 16)
                if 1 <= stage < PAIRS:
                    for u in range(2):
                        sp.wait_ge(x2_step, (r * 2 - 2 + u) * X2S + 2)
                        sp.dma_start(x_res[:, u, :], x_rows[bass.ds((r * 2 + u) * P, P), :]).then_inc(x_res_in, 16)
                if stage >= 2:
                    for u in range(2):
                        sp.wait_ge(o_ready, (r - 2) * 2 + u + 1)
                        sp.dma_start(out_rows[bass.ds(((r - 2) * 2 + u) * P, P), :], o_sb[:, u, :]).then_inc(stored, 16)

            rounds(sp, do_round)
            sp.wait_ge(stored, 16 * TILES)

        @block.gpsimd
        def _(pool):
            pool.memset(ident[:, :], 0.0).then_inc(ident_ready, 1)
            pool.wait_ge(ident_ready, 1)
            pool.affine_select(out=ident[:, :], in_=ident[:, :], compare_op=ALU.not_equal, fill=1.0,
                               base=0, pattern=[[-1, P]], channel_multiplier=1).then_inc(ident_ready, 1)
            pool.memset(minus_half[:, :], -0.5).then_inc(const_ready, 1)
            pool.memset(minus_one[:, :], -1.0).then_inc(const_ready, 1)
            pool.memset(magic_col[:, :], MAGIC).then_inc(const_ready, 1)
            pool.memset(unmagic_col[:, :], -MAGIC).then_inc(const_ready, 1)
            pool.memset(ones[:, :], 1.0).then_inc(const_ready, 1)
            pool.memset(vo[:, :, D:DV], 1.0).then_inc(const_ready, 1)
            pool.dma_start(bk_col[:, :], bk.rearrange("(c p) -> p c", p=P), allow_slow_non_contiguous=True).then_inc(bias_in, 16)
            pool.dma_start(bq_col[:, :], bq.rearrange("(c p) -> p c", p=P), allow_slow_non_contiguous=True).then_inc(bias_in, 16)
            pool.dma_start(bv_col[:, :], bv.rearrange("(c p) -> p c", p=P), allow_slow_non_contiguous=True).then_inc(bias_in, 16)
            pool.dma_start(bo_bc[:, :], bo.partition_broadcast(P)).then_inc(bias_in, 16)
            pool.dma_start(b1_bc[:, :], b1.partition_broadcast(P)).then_inc(bias_in, 16)
            pool.dma_start(b2_bc[:, :], b2.partition_broadcast(P)).then_inc(bias_in, 16)
            pool.wait_ge(const_ready, 6)

            def normalise(j):
                wait_apart(pool, ln1_step, (j + 1) * 4)
                pool.tensor_scalar(ln1_r[:, 0, :], ln1_mv[:, :, 1], EPS, None, ALU.add).then_inc(ln1_row, 1)
                pool.wait_ge(ln1_row, j * 2 + 1)
                pool.tensor_tensor(ln1_r[:, 1, :], ln1_r[:, 0, :], minus_half[:, :], ALU.pow).then_inc(ln1_row, 1)
                wait_apart(pool, ln1_row, j * 2 + 2)
                for u in range(2):
                    pool.tensor_scalar(xn[:, u, :], x_in[:, u, :], ln1_mv[:, u, 0:1], ln1_r[:, 1, u:u + 1],
                                       ALU.subtract, ALU.mult).then_inc(xn_ready, 1)

            def softmax_weights(t, u):
                pool.wait_ge(e_ready, t + 1)
                pool.wait_ge(e_left_ready, t + 1)
                pool.tensor_tensor(e_all[:, u, :], e_all[:, u, :], e_left[:, :], ALU.subtract).then_inc(p_ready, 1)

            def residual(j):
                for u in range(2):
                    if u == 0:
                        pool.wait_ge(x_res_in, (j + 1) * 32)
                        pool.wait_ge(bias_in, 6 * 16)
                    pool.tensor_tensor(x_res[:, u, :], x_res[:, u, :], bo_bc[:, :], ALU.add).then_inc(xb_ready, 1)

            def row_scales_1(j):
                mean_var, base = ln2_mv, j * ROW1
                wait_apart(pool, x2_step, (j + 1) * 2 * X2S)
                n = [0]

                def step(ins):
                    ins.then_inc(row1_step, 1)
                    n[0] += 1
                    wait_apart(pool, row1_step, base + n[0])

                ve, r1, r1s, vn, vne, r2, rr, z, zc, iz, sc, dq = (row1[:, k, :] for k in range(12))
                var = mean_var[:, :, 1]
                step(pool.tensor_scalar(ve, var, EPS, None, ALU.add))
                step(pool.tensor_tensor(r1, ve, minus_half[:, :], ALU.pow))
                step(pool.tensor_tensor(r1s, r1, r1, ALU.mult))
                step(pool.tensor_tensor(vn, r1s, var, ALU.mult))
                step(pool.tensor_scalar(vne, vn, EPS, None, ALU.add))
                step(pool.tensor_tensor(r2, vne, minus_half[:, :], ALU.pow))
                step(pool.tensor_tensor(rr, r1, r2, ALU.mult))
                step(pool.tensor_tensor(z, rr, cen_max[:, :], ALU.mult))
                step(pool.tensor_scalar(zc, z, 1e-5, None, ALU.max))
                step(pool.tensor_tensor(iz, zc, minus_one[:, :], ALU.pow))
                step(pool.tensor_scalar(iz, iz, 127.0, None, ALU.mult))
                step(pool.tensor_tensor(sc, iz, rr, ALU.mult))
                step(pool.tensor_scalar(dq, zc, 1.0 / 127.0, wmean[:, 0:1], ALU.mult, ALU.mult))

            def quantise_1(j):
                for u in range(2):
                    pool.tensor_scalar(y1[:, u, :], cen[:, u, :], row1[:, 10, u:u + 1], MAGIC,
                                       ALU.mult, ALU.add).then_inc(y1_ready, 1)

            def keep_residual(j):
                for u in range(2):
                    pool.tensor_tensor(x2b[:, u, :], x2[:, u, :], b2_bc[:, :], ALU.add).then_inc(x2b_ready, 1)

            def row_scales_2(j):
                base = j * ROW2
                pool.wait_ge(g_sq_ready, (j + 1) * 2)
                wait_apart(pool, g_max_ready, (j + 1) * 2)
                n = [0]

                def step(ins):
                    ins.then_inc(row2_step, 1)
                    n[0] += 1
                    wait_apart(pool, row2_step, base + n[0])

                ms, r, z, zc, iz, iz2, sc, dq = (row2[:, k, :] for k in range(8))
                step(pool.tensor_scalar(ms, g_ssq[:, :], 1.0 / F, EPS, ALU.mult, ALU.add))
                step(pool.tensor_tensor(r, ms, minus_half[:, :], ALU.pow))
                step(pool.tensor_tensor(z, r, g_max[:, :], ALU.mult))
                step(pool.tensor_scalar(zc, z, 1e-5, None, ALU.max))
                step(pool.tensor_tensor(iz, zc, minus_one[:, :], ALU.pow))
                step(pool.tensor_scalar(iz2, iz, 127.0, None, ALU.mult))
                step(pool.tensor_tensor(sc, iz2, r, ALU.mult))
                step(pool.tensor_scalar(dq, zc, 1.0 / 127.0, wmean[:, 1:2], ALU.mult, ALU.mult))

            normalise(0)
            residual(0)
            pool.wait_ge(wscale_step, 2)

            def do_round(r, stage):
                if 1 <= stage <= PAIRS:
                    softmax_weights(r * 2 - 1, 1)
                if 2 <= stage:
                    row_scales_2(r - 2)
                if stage + 1 < PAIRS:
                    if stage >= 1:
                        pass
                    pool.wait_ge(q_ready, (r + 1) * DC)
                    normalise(r + 1)
                if 1 <= stage <= PAIRS:
                    row_scales_1(r - 1)
                    quantise_1(r - 1)
                if stage < PAIRS:
                    softmax_weights(r * 2, 0)
                if 1 <= stage <= PAIRS:
                    if stage >= 2:
                        pool.wait_ge(o_ready, (r - 1) * 2)
                    keep_residual(r - 1)
                if 1 <= stage < PAIRS:
                    residual(r)

            rounds(pool, do_round)

        @block.scalar
        def _(act):
            def taken(n, dst, src, **how):
                act.wait_ge(prep_ready, n + 1)
                act.activation(dst, src, ACT.Identity, **how).then_inc(prep_taken, 1)

            def bank(n):
                return prep[n % 4]

            def copy_scores(t, u, c):
                at, n = CHUNKS[c]
                act.wait_ge(s_ready, t * SC + c + 1)
                act.activation(s_sb[:, u, at:at + n], score[c][:, 0:n], ACT.Copy).then_inc(s_copied, 1)

            def buffer_free(t, u):
                act.wait_ge(topk_step, (t - 2) * STEPS + 2)
                act.wait_ge(e_ready, t - 1)

            act.wait_ge(const_ready, 6)
            for k, n in enumerate("kq"):
                taken(JOB_WQK + k, WT[n][:, :, :], bank(JOB_WQK + k)[:, :].rearrange("p (c o) -> p c o", c=DC))
            for k in range(NCTX):
                n = min(2 * P, S - 2 * k * P)
                src = bank(JOB_CTX + k)[:, :].rearrange("p (c s) -> p c s", c=DC)[:, :, 0:n]
                taken(JOB_CTX + k, ctxT[:, :, 2 * k * P:2 * k * P + n], src)
            act.wait_ge(bias_in, 6 * 16)
            for k in range(SC * DC):
                (at, n), o = CHUNKS[k // DC], k % DC
                taken(JOB_K + k, kT[:, o, at:at + n], bank(JOB_K + k)[:, 0:n], bias=bk_col[:, o:o + 1])
            taken(JOB_Q0, xnT[:, :, :], bank(JOB_Q0)[:, :].rearrange("p (c t) -> p c t", c=DC))
            act.wait_ge(prep_ready, JOB_Q0 + 2)
            for o in range(DC):
                act.activation(qT[:, o, :], bank(JOB_Q0 + 1)[:, o * 2 * P:(o + 1) * 2 * P], ACT.Identity,
                               bias=bq_col[:, o:o + 1]).then_inc(q_ready, 1)
            for c in range(SC):
                copy_scores(0, 0, c)
            for c in range(SC):
                copy_scores(1, 1, c)
            for k, n in enumerate("vo"):
                taken(JOB_WVO + k, WT[n][:, :, :], bank(JOB_WVO + k)[:, :].rearrange("p (c o) -> p c o", c=DC))
            for k in range(SC * DC):
                (at, n), o = CHUNKS[k // DC], k % DC
                if k == 0:
                    act.wait_ge(prep_ready, JOB_K)
                taken(JOB_V + k, vT[:, o, at:at + n], bank(JOB_V + k)[:, 0:n], bias=bv_col[:, o:o + 1])
            for k in range(NCTX):
                nb = min(2, SB - 2 * k)
                rows = P if 2 * k + nb < SB else S_LAST
                taken(JOB_VO + k, vo[0:rows, 2 * k:2 * k + nb, 0:D],
                      bank(JOB_VO + k)[0:rows, 0:nb * D].rearrange("p (b d) -> p b d", b=nb))
            for k in range(4):
                b = k % 2 * 4
                taken(JOB_W1 + k, w1T[:, k // 2, b * P:(b + 4) * P], bank(JOB_W1 + k)[:, :], bias=unmagic_col[:, 0:1])
            for k in range(4):
                c, b = k // 2, k % 2 * 4
                taken(JOB_W2 + k, w2T[:, b:b + 4, c * P:(c + 1) * P],
                      bank(JOB_W2 + k)[:, :].rearrange("p (b o) -> p b o", b=4), bias=unmagic_col[:, 0:1])

            turns = Count(TURNS)

            def take_turn(dst, cols, parts=1, bias=None):
                k = turns.before % 2
                act.wait_ge(turned, turns.next() + 1)
                src = turn[k][0:dst.shape[0], 0:cols]
                if parts > 1:
                    src = src.rearrange("p (b n) -> p b n", b=parts)
                if bias is None:
                    act.activation(dst, src, ACT.Copy).then_inc(turn_taken, 1)
                else:
                    act.activation(dst, src, ACT.Identity, bias=bias).then_inc(turn_taken, 1)

            def take_weights(q):
                lo, hi = QUADS[q]
                rows = P if hi < SB else S_LAST
                take_turn(pT[0:rows, lo * P:hi * P], (hi - lo) * P)

            def exp_left(t, u):
                act.wait_ge(topk_step, (t + 1) * STEPS)
                if u or not isinstance(t, int) or t > 0:
                    act.wait_ge(p_ready, t)
                act.activation(e_left[:, :], s_left[:, u, :], ACT.Exp, bias=neg_max[:, u:u + 1],
                               scale=SCALE).then_inc(e_left_ready, 1)

            def exp_all(t, u, old):
                act.wait_ge(max_ready, t + 1)
                if old:
                    act.wait_ge(turned, old)
                act.activation(e_all[:, u, :], s_sb[:, u, :], ACT.Exp, bias=neg_max[:, u:u + 1],
                               scale=SCALE).then_inc(e_ready, 1)

            def do_round(r, stage):
                if 1 <= stage <= PAIRS:
                    exp_left(r * 2 - 1, 1)
                if 1 <= stage < PAIRS:
                    buffer_free(r * 2 + 1, 1)
                    for c in range(SC):
                        copy_scores(r * 2 + 1, 1, c)
                if stage + 1 < PAIRS:
                    take_turn(xnT[:, :, :], 2 * D, DC)
                if stage < PAIRS:
                    exp_all(r * 2, 0, None)
                if 1 <= stage <= PAIRS:
                    for q in range(NT):
                        take_weights(q)
                if stage >= 2:
                    act.wait_ge(row2_step, (r - 1) * ROW2)
                    for u in range(2):
                        act.activation(y2[:, u, :], g[:, u, :], ACT.Identity, scale=row2[:, 6, u:u + 1],
                                       bias=magic_col[:, 0:1]).then_inc(y2_ready, 1)
                    for u in range(2):
                        for h in range(2):
                            take_turn(y2T[:, h * 4:h * 4 + 4, u * P:(u + 1) * P], BANK, 4, unmagic_col[:, 0:1])
                if stage < PAIRS:
                    exp_left(r * 2, 0)
                if stage + 1 < PAIRS:
                    buffer_free(r * 2 + 2, 0)
                    for c in range(SC):
                        copy_scores(r * 2 + 2, 0, c)
                if 1 <= stage <= PAIRS:
                    take_turn(y1T[:, :, :], 2 * D, DC, unmagic_col[:, 0:1])
                if stage < PAIRS:
                    exp_all(r * 2 + 1, 1, None)
                    for q in range(NT):
                        take_weights(q)
                if 1 <= stage <= PAIRS:
                    for u in range(2):
                        act.wait_ge(h_ready, ((r - 1) * 2 + u + 1) * 2)
                        act.activation(g[:, u, :], g[:, u, :], ACT.Gelu).then_inc(g_ready, 1)
                    for u in range(2):
                        act.wait_ge(g_ready, (r - 1) * 2 + u + 1)
                        if u or stage >= 2:
                            act.wait_ge(g_sq_ready, (r - 1) * 2 + u)
                        act.activation(g_sq[:, :], g[:, u, :], ACT.Square,
                                       accum_out=g_ssq[:, u:u + 1]).then_inc(g_sq_ready, 1)

            rounds(act, do_round, [turns])

        @block.vector
        def _(dve):
            def ln1_stats(j):
                dve.wait_ge(x_in_done, (j + 1) * 32)
                for u in range(2):
                    dve.bn_stats(ln1_part[:, u, :], x_in[:, u, :]).then_inc(ln1_step, 1)
                for u in range(2):
                    wait_apart(dve, ln1_step, j * 4 + u + 1)
                    dve.bn_aggr(ln1_mv[:, u, :], ln1_part[:, u, :]).then_inc(ln1_step, 1)

            def topk_round(t, u, k):
                src = s_left if k else s_sb
                if k == 0:
                    wait_apart(dve, s_copied, (t + 1) * SC)
                else:
                    wait_apart(dve, topk_step, t * STEPS + 2 * k)
                dve.max(best[:, u, k, :], src[:, u, :]).then_inc(topk_step, 1)
                wait_apart(dve, topk_step, t * STEPS + 2 * k + 1)
                dve.match_replace(s_left[:, u, :], best[:, u, k, :], src[:, u, :], LOWEST).then_inc(topk_step, 1)
                if k == 0:
                    dve.tensor_scalar(neg_max[:, u:u + 1], best[:, u, 0, 0:1], -SCALE, None,
                                      ALU.mult).then_inc(max_ready, 1)

            results = Count(RESULTS)

            def take_result():
                k = results.before % 2
                dve.wait_ge(result_ready, results.next() + 1)
                return result[k]

            def queries(j):
                bank = take_result()
                for o in range(DC):
                    dve.tensor_scalar(qT[:, o, :], bank[:, o * 2 * P:(o + 1) * 2 * P], bq_col[:, o:o + 1], None,
                                      ALU.add).then_inc(q_ready, 1)
                dve.wait_ge(q_ready, (j + 1) * DC)
                dve.nop().then_inc(result_taken, 1)

            def attended(t, u):
                base = t * X2S
                bank = take_result()
                dve.wait_ge(xb_ready, t + 1)
                dve.reciprocal(inv_sum[:, u:u + 1], bank[:, D:DV]).then_inc(x2_step, 1)
                dve.wait_ge(x2_step, base + 1)
                dve.scalar_tensor_tensor(x2[:, u, :], bank[:, 0:D], inv_sum[:, u:u + 1], x_res[:, u, :],
                                         ALU.mult, ALU.add).then_inc(x2_step, 1)
                dve.wait_ge(x2_step, base + 2)
                dve.bn_stats(ln2_part[:, u, :], x2[:, u, :]).then_inc(x2_step, 1)
                wait_apart(dve, x2_step, base + 3)
                dve.bn_aggr(ln2_mv[:, u, :], ln2_part[:, u, :]).then_inc(x2_step, 1)
                dve.wait_ge(x2_step, base + 4)
                dve.tensor_scalar(cen[:, u, :], x2[:, u, :], ln2_mv[:, u, 0:1], None,
                                  ALU.subtract).then_inc(x2_step, 1)
                dve.wait_ge(x2_step, base + 5)
                dve.tensor_reduce(cen_max[:, u:u + 1], cen[:, u, :], AX.X, ALU.max, apply_absolute_value=True).then_inc(x2_step, 1)
                dve.wait_ge(x2_step, base + 6)
                dve.nop().then_inc(x2_step, 1)
                dve.nop().then_inc(result_taken, 1)

            def hidden(j):
                dve.wait_ge(row1_step, (j + 1) * ROW1)
                for u in range(2):
                    for h in range(2):
                        bank = take_result()
                        dve.scalar_tensor_tensor(g[:, u, h * BANK:(h + 1) * BANK], bank[:, :], row1[:, 11, u:u + 1],
                                                 b1_bc[:, h * BANK:(h + 1) * BANK], ALU.mult,
                                                 ALU.add).then_inc(h_ready, 1)
                        dve.wait_ge(h_ready, j * 4 + u * 2 + h + 1)
                        dve.nop().then_inc(result_taken, 1)

            def gelu_max(j):
                for u in range(2):
                    dve.wait_ge(g_ready, j * 2 + u + 1)
                    dve.tensor_reduce(g_max[:, u:u + 1], g[:, u, :], AX.X, ALU.max, apply_absolute_value=True).then_inc(g_max_ready, 1)

            def outputs(j):
                bank = take_result()
                dve.wait_ge(x2b_ready, (j + 1) * 2)
                if not isinstance(j, int) or j > 0:
                    dve.wait_ge(stored, j * 32)
                for u in range(2):
                    dve.scalar_tensor_tensor(o_sb[:, u, :], bank[:, u * D:(u + 1) * D], row2[:, 7, u:u + 1],
                                             x2b[:, u, :], ALU.mult, ALU.add).then_inc(o_ready, 1)
                dve.wait_ge(o_ready, (j + 1) * 2)
                dve.nop().then_inc(result_taken, 1)

            ln1_stats(0)
            dve.wait_ge(wff_in, 32)
            for k, w in enumerate((w1_sb, w2_sb)):
                dve.tensor_reduce(wsum[:, k:k + 1], w[:, :, :], AX.XY, ALU.add,
                                  apply_absolute_value=True).then_inc(wsum_ready, 1)
            dve.wait_ge(prep_ready, JOB_MEAN + 1)
            dve.tensor_scalar(wmean[:, :], prep[JOB_MEAN % 4][:, 0:2], 1.0 / (D * F), 1e-5,
                              ALU.mult, ALU.max).then_inc(wscale_step, 1)
            dve.wait_ge(wscale_step, 1)
            dve.reciprocal(winv[:, :], wmean[:, :]).then_inc(wscale_step, 1)
            dve.wait_ge(wscale_step, 2)
            for k, w in enumerate((w1_sb, w2_sb)):
                dve.tensor_scalar(w[:, :, :], w[:, :, :], winv[:, k:k + 1], MAGIC, ALU.mult,
                                  ALU.add).then_inc(wscale_step, 1)
                dve.wait_ge(wscale_step, 3 + k)
                dve.tensor_scalar(w[:, :, :], w[:, :, :], MAGIC + 1.0, MAGIC - 1.0, ALU.min,
                                  ALU.max).then_inc(ternary_ready, 1)

            def do_round(r, stage):
                if 2 <= stage:
                    gelu_max(r - 2)
                if stage + 1 < PAIRS:
                    ln1_stats(r + 1)
                if stage < PAIRS:
                    topk_round(r * 2, 0, 0)
                if 1 <= stage <= PAIRS:
                    attended(r * 2 - 2, 0)
                if stage < PAIRS:
                    topk_round(r * 2, 0, 1)
                if stage + 1 < PAIRS:
                    queries(r + 1)
                if stage < PAIRS:
                    topk_round(r * 2, 0, 2)
                    topk_round(r * 2, 0, 3)
                if 1 <= stage <= PAIRS:
                    attended(r * 2 - 1, 1)
                if stage < PAIRS:
                    topk_round(r * 2 + 1, 1, 0)
                if stage >= 2:
                    outputs(r - 2)
                if stage < PAIRS:
                    topk_round(r * 2 + 1, 1, 1)
                if 1 <= stage <= PAIRS:
                    hidden(r - 1)
                if stage < PAIRS:
                    topk_round(r * 2 + 1, 1, 2)
                    topk_round(r * 2 + 1, 1, 3)

            rounds(dve, do_round, [results])

        @block.tensor
        def _(pe):
            def prep_bank(n):
                if n >= 4:
                    pe.wait_ge(prep_taken, taken_before(n - 3))
                return prep[n % 4]

            def taken_before(n):
                return n - (n > JOB_Q0 + 1) - (n > JOB_MEAN)

            def prep_turn(n, blocks):
                bank = prep_bank(n)
                for k, (src, at) in enumerate(blocks):
                    rows = src.shape[0]
                    ins = pe.transpose(bank[:, at:at + rows], src, ident[0:rows, 0:rows])
                ins.then_inc(prep_ready, 1)

            def weights_T(n, name):
                prep_turn(n, [(W4[name][:, o, c * P:(c + 1) * P], c * D + o * P) for c in range(DC) for o in range(DC)])

            def project(n0, w):
                for k in range(SC * DC):
                    (at, n), o = CHUNKS[k // DC], k % DC
                    bank = prep_bank(n0 + k)
                    for c in range(DC):
                        ins = pe.matmul(bank[:, 0:n], WT[w][:, c, o * P:(o + 1) * P], ctxT[:, c, at:at + n],
                                        start=(c == 0), stop=(c == DC - 1))
                    ins.then_inc(prep_ready, 1)

            def scores(t, u, c):
                at, n = CHUNKS[c]
                if u or not isinstance(t, int) or t > 0:
                    pe.wait_ge(s_copied, (t - 1) * SC + c + 1)
                for k in range(DC):
                    ins = pe.matmul(score[c][:, 0:n], qT[:, k, u * P:(u + 1) * P], kT[:, k, at:at + n],
                                    start=(k == 0), stop=(k == DC - 1))
                ins.then_inc(s_ready, 1)

            pe.wait_ge(ident_ready, 2)
            pe.wait_ge(wqk_in, 32)
            weights_T(JOB_WQK, "k")
            weights_T(JOB_WQK + 1, "q")
            for k in range(NCTX):
                if k == 0:
                    pe.wait_ge(ctx_in, 48)
                blocks = []
                for b in range(2 * k, min(2 * k + 2, SB)):
                    rows = P if b < SB - 1 else S_LAST
                    blocks += [(ctx_sb[0:rows, b, c * P:(c + 1) * P], c * D + (b - 2 * k) * P) for c in range(DC)]
                prep_turn(JOB_CTX + k, blocks)
            pe.wait_ge(prep_taken, JOB_K)
            project(JOB_K, "k")
            pe.wait_ge(xn_ready, 2)
            prep_turn(JOB_Q0, [(xn[:, u, c * P:(c + 1) * P], c * D + u * P) for c in range(DC) for u in range(2)])
            bank = prep_bank(JOB_Q0 + 1)
            pe.wait_ge(prep_taken, JOB_Q0 + 1)
            for o in range(DC):
                for c in range(DC):
                    ins = pe.matmul(bank[:, o * 2 * P:(o + 1) * 2 * P], WT["q"][:, c, o * P:(o + 1) * P], xnT[:, c, :],
                                    start=(c == 0), stop=(c == DC - 1))
            ins.then_inc(prep_ready, 1)
            pe.wait_ge(q_ready, DC)
            for c in range(SC):
                scores(0, 0, c)
            for c in range(SC):
                scores(1, 1, c)
            pe.wait_ge(wvo_in, 32)
            weights_T(JOB_WVO, "v")
            weights_T(JOB_WVO + 1, "o")
            pe.wait_ge(prep_taken, taken_before(JOB_V))
            project(JOB_V, "v")
            pe.wait_ge(prep_taken, taken_before(JOB_VO))
            for k in range(NCTX):
                bank = prep_bank(JOB_VO + k)
                for b in range(2 * k, min(2 * k + 2, SB)):
                    rows = P if b < SB - 1 else S_LAST
                    at = (b - 2 * k) * D
                    for c in range(DC):
                        ins = pe.matmul(bank[0:rows, at:at + D], vT[:, c, b * P:b * P + rows], WT["o"][:, c, :],
                                        start=(c == 0), stop=(c == DC - 1))
                ins.then_inc(prep_ready, 1)
            pe.wait_ge(wsum_ready, 2)
            pe.wait_ge(const_ready, 6)
            pe.matmul(prep_bank(JOB_MEAN)[:, 0:2], ones[:, :], wsum[:, :], start=True, stop=True).then_inc(prep_ready, 1)
            pe.wait_ge(ternary_ready, 1)
            for k in range(4):
                c, b = k // 2, k % 2 * 4
                if k == 3:
                    pe.wait_ge(wscale_step, 1)
                prep_turn(JOB_W1 + k, [(w1_sb[:, b + i, c * P:(c + 1) * P], i * P) for i in range(4)])
            pe.wait_ge(ternary_ready, 2)
            for k in range(4):
                c, b = k // 2, k % 2 * 4
                prep_turn(JOB_W2 + k, [(w2_sb[:, c, (b + i) * P:(b + i + 1) * P], i * P) for i in range(4)])
            pe.wait_ge(prep_taken, taken_before(PREPS))

            turns, results = Count(TURNS), Count(RESULTS)

            def turn_bank():
                k, first = turns.before % 2, turns.loop is None and turns.before < 2
                n = turns.next()
                if not first:
                    pe.wait_ge(turn_taken, n - 1)
                return turn[k]

            def result_bank():
                k, first = results.before % 2, results.loop is None and results.before < 2
                n = results.next()
                if not first:
                    pe.wait_ge(result_taken, n - 1)
                return result[k]

            def turn_weights(u, q):
                bank = turn_bank()
                lo, hi = QUADS[q]
                for b in range(lo, hi):
                    n = P if b < SB - 1 else S_LAST
                    ins = pe.transpose(bank[0:n, (b - lo) * P:(b - lo + 1) * P],
                                       e_all[:, u, b * P:b * P + n], ident[:, :])
                ins.then_inc(turned, 1)

            def weighted(bank, q, landed):
                pe.wait_ge(turn_taken, landed)
                lo, hi = QUADS[q]
                for b in range(lo, hi):
                    n = P if b < SB - 1 else S_LAST
                    ins = pe.matmul(bank[:, 0:DV], pT[0:n, b * P:(b + 1) * P], vo[0:n, b, :],
                                    start=(b == 0), stop=(b == SB - 1))
                return ins

            def turn_y2(u, h):
                bank = turn_bank()
                for k in range(4):
                    ins = pe.transpose(bank[:, k * P:(k + 1) * P], y2[:, u, (h * 4 + k) * P:(h * 4 + k + 1) * P],
                                       ident[:, :])
                ins.then_inc(turned, 1)

            def turn_pair(src):
                bank = turn_bank()
                for c in range(DC):
                    for u in range(2):
                        ins = pe.transpose(bank[:, c * D + u * P:c * D + (u + 1) * P], src[:, u, c * P:(c + 1) * P],
                                           ident[:, :])
                ins.then_inc(turned, 1)

            def turned_so_far():
                n = turns.before
                return n if turns.loop is None else (turns.loop - LOOP[0]) * TURNS + n

            def do_round(r, stage):
                if 1 <= stage < PAIRS:
                    for c in range(SC):
                        scores(r * 2 + 1, 1, c)
                if stage + 1 < PAIRS:
                    pe.wait_ge(xn_ready, (r + 2) * 2)
                    turn_pair(xn)
                    bank = result_bank()
                    pe.wait_ge(turn_taken, turned_so_far())
                    for o in range(DC):
                        for c in range(DC):
                            ins = pe.matmul(bank[:, o * 2 * P:(o + 1) * 2 * P], WT["q"][:, c, o * P:(o + 1) * P],
                                            xnT[:, c, :], start=(c == 0), stop=(c == DC - 1))
                    ins.then_inc(result_ready, 1)
                if 1 <= stage <= PAIRS:
                    pe.wait_ge(p_ready, r * 2)
                    landed = turned_so_far()
                    for q in range(NT):
                        turn_weights(1, q)
                    bank = result_bank()
                    for q in range(NT):
                        ins = weighted(bank, q, landed + q + 1)
                    ins.then_inc(result_ready, 1)
                if stage >= 2:
                    for u in range(2):
                        pe.wait_ge(y2_ready, (r - 2) * 2 + u + 1)
                        for h in range(2):
                            turn_y2(u, h)
                    bank = result_bank()
                    for u in range(2):
                        pe.wait_ge(turn_taken, turned_so_far() - 2 + 2 * u)
                        for b in range(FB):
                            ins = pe.matmul(bank[:, u * D:(u + 1) * D], y2T[:, b, u * P:(u + 1) * P], w2T[:, b, :],
                                            start=(b == 0), stop=(b == FB - 1))
                    ins.then_inc(result_ready, 1)
                if stage + 1 < PAIRS:
                    pe.wait_ge(q_ready, (r + 2) * DC)
                    for c in range(SC):
                        scores(r * 2 + 2, 0, c)
                if 1 <= stage <= PAIRS:
                    pe.wait_ge(y1_ready, r * 2)
                    turn_pair(y1)
                    landed = turned_so_far()
                    for u in range(2):
                        for h in range(2):
                            bank = result_bank()
                            if u == h == 0:
                                pe.wait_ge(turn_taken, landed)
                            for c in range(DC):
                                ins = pe.matmul(bank[:, :], y1T[:, c, u * P:(u + 1) * P],
                                                w1T[:, c, h * BANK:(h + 1) * BANK], start=(c == 0), stop=(c == DC - 1))
                            ins.then_inc(result_ready, 1)
                if stage < PAIRS:
                    pe.wait_ge(p_ready, r * 2 + 1)
                    landed = turned_so_far()
                    for q in range(NT):
                        turn_weights(0, q)
                    bank = result_bank()
                    for q in range(NT):
                        ins = weighted(bank, q, landed + q + 1)
                    ins.then_inc(result_ready, 1)

            rounds(pe, do_round, [turns, results])


_INS = ["x", "ctx_1024", "L0_xattn_Wq", "L0_xattn_bq", "L0_xattn_Wk", "L0_xattn_bk", "L0_xattn_Wv", "L0_xattn_bv",
        "L0_xattn_Wo", "L0_xattn_bo", "L0_ffn_w1", "L0_ffn_b1", "L0_ffn_w2", "L0_ffn_b2"]


def kernel(**inputs):
    from concourse import bacc
    from concourse.bass_utils import run_bass_kernel_spmd

    nc = bacc.Bacc("TRN2", target_bir_lowering=False, num_devices=1)
    arrays, args = {}, []
    for name in _INS:
        a = np.ascontiguousarray(inputs[name])
        arrays[f"in_{name}"] = a
        args.append(nc.dram_tensor(f"in_{name}", a.shape, mybir.dt.from_np(a.dtype), kind="ExternalInput").ap())
    args.append(nc.dram_tensor("out", (1, T, D), F32, kind="ExternalOutput").ap())
    build(nc, *args)
    r = run_bass_kernel_spmd(nc, [arrays], core_ids=[0])
    return r.results[0]["out"]
```

```python
from contextlib import ExitStack

import numpy as np

import concourse.bass as bass
from concourse import mybir

F32 = mybir.dt.float32
BF16 = mybir.dt.bfloat16
ALU = mybir.AluOpType
ACT = mybir.ActivationFunctionType
AX = mybir.AxisListType

P = 128
D = 256
DC = D // P
T = 2048
S = 1601
F = 1024
FB = F // P
BANK = 512
TOPK = 32
ROUNDS = TOPK // 8
TILES = T // P
PAIRS = TILES // 2
SB = -(-S // P)
S_LAST = S - (SB - 1) * P
SC = -(-S // BANK)
CHUNKS = [(c * BANK, min(BANK, S - c * BANK)) for c in range(SC)]
QUADS = [(g, min(g + 4, SB)) for g in range(0, SB, 4)]
NT = len(QUADS)
DV = D + 1
SCALE = float(D) ** -0.5
EPS = 1e-5
LOWEST = -3.4028234e38
MAGIC = 12582912.0
PIECE = 50
PIECES = S // PIECE
CAND = 8 * PIECES

TURNS = 1 + 2 + NT + 4 + 1 + NT
RESULTS = 1 + 1 + 2 + 4
LOOP = (2, PAIRS - 2)
LAST_ROUND = PAIRS + 2


class Count:

    def __init__(self, per_round):
        self.per_round, self.before, self.loop = per_round, 0, None

    def next(self):
        n = self.before
        self.before += 1
        return n if self.loop is None else (self.loop - LOOP[0]) * self.per_round + n

    def enter(self, register):
        self.loop, self.entry = register, self.before

    def leave(self):
        assert self.before == self.entry + self.per_round
        self.loop = None
        self.before = self.entry + self.per_round * (LOOP[1] - LOOP[0])


def rounds(engine, do_round, counts=()):
    for r in range(LOOP[0]):
        do_round(r, r)
    with engine.Fori(LOOP[0], LOOP[1]) as r:
        for c in counts:
            c.enter(r)
        do_round(r, LOOP[0])
        for c in counts:
            c.leave()
    for r in range(LOOP[1], LAST_ROUND):
        do_round(r, r)


def build(nc, x, ctx, Wq, bq, Wk, bk, Wv, bv, Wo, bo, w1, b1, w2, b2, out):
    x_rows = x.rearrange("a t d -> (a t) d")
    out_rows = out.rearrange("a t d -> (a t) d")
    ctx_rows = ctx.rearrange("a s d -> (a s) d")

    with ExitStack() as stack:
        def sb(name, shape, dt=F32):
            return stack.enter_context(nc.sbuf_tensor(name, shape, dt))

        def sem(name):
            return stack.enter_context(nc.semaphore(name))

        score = [stack.enter_context(nc.psum_tensor(f"score{c}", [P, BANK], F32)) for c in range(SC)]
        turn = [stack.enter_context(nc.psum_tensor(f"turn{c}", [P, BANK], F32)) for c in range(2)]
        result = [stack.enter_context(nc.psum_tensor(f"result{c}", [P, BANK], F32)) for c in range(2)]
        prep = turn + result

        W4 = {n: sb(f"w_{n}", [P, DC, D]) for n in "qkvo"}
        WT = {n: sb(f"wt_{n}", [P, DC, D]) for n in "qko"}
        wvoT = sb("wvoT", [P, DC, D])
        bv_bc = sb("bv_bc", [P, DC, P])
        w1_sb = sb("w1_sb", [P, FB, D])
        w2_sb = sb("w2_sb", [P, DC, F])
        w1T = sb("w1T", [P, DC, F], BF16)
        w2T = sb("w2T", [P, FB, D], BF16)
        bq_col, bk_col, bv_col = (sb(n, [P, DC]) for n in ("bq_col", "bk_col", "bv_col"))
        bo_bc = sb("bo_bc", [P, D])
        bvo_bc = sb("bvo_bc", [P, D])
        b1_bc = sb("b1_bc", [P, F])
        b2_bc = sb("b2_bc", [P, D])
        ident = sb("ident", [P, P])
        ones = sb("ones", [P, P])
        wsum = sb("wsum", [P, 2])
        wmean = sb("wmean", [P, 2])
        winv = sb("winv", [P, 2])
        minus_half = sb("minus_half", [P, 2])
        minus_one = sb("minus_one", [P, 2])
        magic_col = sb("magic_col", [P, 1])
        unmagic_col = sb("unmagic_col", [P, 1])

        ctx_sb = sb("ctx_sb", [P, SB, D])
        ctxT = sb("ctxT", [P, DC, S])
        kT = sb("kT", [P, DC, S])
        vo = sb("vo", [P, SB, DV])

        x_in = sb("x_in", [P, 2, D])
        ln1_part = sb("ln1_part", [P, 2, 6])
        ln1_mv = sb("ln1_mv", [P, 2, 2])
        ln1_r = sb("ln1_r", [P, 2, 2])
        xn = sb("xn", [P, 2, D])
        xnT = sb("xnT", [P, DC, 2 * P])
        qT = sb("qT", [P, DC, 2 * P])

        s_sb = sb("s_sb", [P, 2, S])
        cand = sb("cand", [P, 2, CAND])
        cand_left = sb("cand_left", [P, CAND])
        cand_ge = sb("cand_ge", [P, CAND], BF16)
        best = sb("best", [P, ROUNDS, 8])
        counts = sb("counts", [P, 2])
        doubt = sb("doubt", [P, 32])
        doubt_row = sb("doubt_row", [P, P])
        doubtful = sb("doubtful", [1, 2], mybir.dt.int32)
        s_left = sb("s_left", [P, S])
        best_of_all = sb("best_of_all", [P, 8])
        neg_max = sb("neg_max", [P, 2])
        e_all = sb("e_all", [P, 2, S])
        pT = sb("pT", [P, SB * P])
        inv_sum = sb("inv_sum", [P, 2])
        x_res = sb("x_res", [P, 2, D])
        x2 = sb("x2", [P, 2, D])

        ln2_part = sb("ln2_part", [P, 2, 6])
        ln2_mv = sb("ln2_mv", [P, 2, 2])
        cen = sb("cen", [P, 2, D])
        cen_max = sb("cen_max", [P, 2])
        row1 = sb("row1", [P, 12, 2])
        y1 = sb("y1", [P, 2, D])
        y1T = sb("y1T", [P, DC, 2 * P], BF16)
        g = sb("g", [P, 2, F])
        g_sq = sb("g_sq", [P, F], BF16)
        g_ssq = sb("g_ssq", [P, 2])
        g_max = sb("g_max", [P, 2])
        row2 = sb("row2", [P, 8, 2])
        y2 = sb("y2", [P, 2, F])
        y2T = sb("y2T", [P, FB, 2 * P], BF16)
        x2b = sb("x2b", [P, 2, D])
        o_sb = sb("o_sb", [P, 2, D])

        wqk_in, wvo_in, ctx_in, wff_in, bias_in = (sem(n) for n in ("wqk_in", "wvo_in", "ctx_in", "wff_in", "bias_in"))
        x_in_done, stored = sem("x_in_done"), sem("stored")
        x_res_in = [sem("x_res_in_0"), sem("x_res_in_1")]
        bv_spread, doubt_cleared = sem("bv_spread"), sem("doubt_cleared")
        const_ready, ident_ready = sem("const_ready"), sem("ident_ready")
        prep_ready, prep_taken = sem("prep_ready"), sem("prep_taken")
        wsum_ready, ternary_ready, wscale_step = sem("wsum_ready"), sem("ternary_ready"), sem("wscale_step")
        ln1_step, ln1_row, xn_ready, q_ready = sem("ln1_step"), sem("ln1_row"), sem("xn_ready"), sem("q_ready")
        s_ready, s_copied, cand_ready, max_ready = sem("s_ready"), sem("s_copied"), sem("cand_ready"), sem("max_ready")
        topk_step, settle_step, general_step = sem("topk_step"), sem("settle_step"), sem("general_step")
        e_ready, masked, p_ready = sem("e_ready"), sem("masked"), sem("p_ready")
        turned, turn_taken, xn_turned = sem("turned"), sem("turn_taken"), sem("xn_turned")
        result_ready, result_taken = sem("result_ready"), sem("result_taken")
        x2_step, xb_ready, bo_ready = sem("x2_step"), sem("xb_ready"), sem("bo_ready")
        row1_step, y1_ready, x2b_ready = sem("row1_step"), sem("y1_ready"), sem("x2b_ready")
        g_ready, g_sq_ready, g_max_ready = sem("g_ready"), sem("g_sq_ready"), sem("g_max_ready")
        row2_step, y2_ready = sem("row2_step"), sem("y2_ready")

        JOB_WQK = 0
        JOB_CTX = JOB_WQK + 2
        NCTX = -(-SB // 2)
        JOB_K = JOB_CTX + NCTX
        JOB_MEAN = JOB_K + SC * DC
        JOB_Q0 = JOB_MEAN + 1
        JOB_WO = JOB_Q0 + 2
        JOB_WVO = JOB_WO + 1
        JOB_BVO = JOB_WVO + 1
        JOB_VO = JOB_BVO + 1
        JOB_W1 = JOB_VO + NCTX
        JOB_W2 = JOB_W1 + 4
        PREPS = JOB_W2 + 4

        PREPS_BVO = JOB_BVO + 1 - 2
        ROW1, ROW2, X2S = 13, 8, 5


        def taken_h(j, u):
            last = isinstance(j, int) and j == PAIRS - 1
            return j * RESULTS + (4 if last else 5) + 2 * u

        def taken_out(j, u):
            last = isinstance(j, int) and j == PAIRS - 1
            return j * RESULTS + (7 if last else 9) + u

        waits_passed = {"pool": sem("pool_waits_passed"), "dve": sem("dve_waits_passed")}

        def wait_apart(engine, semaphore, value):
            engine.wait_ge(semaphore, value)
            if not isinstance(value, int):
                engine.sem_inc(waits_passed["pool" if engine.engine == nc.gpsimd.engine else "dve"], 1)

        block = stack.enter_context(nc.Block())

        @block.sync
        def _(sp):
            def w_load(n, W, s):
                sp.dma_start(W4[n][:, :, :], W.rearrange("(c p) d -> p c d", p=P)).then_inc(s, 16)

            w_load("k", Wk, wqk_in)
            w_load("q", Wq, wqk_in)
            full = SB - 1
            half = full // 2
            sp.dma_start(ctx_sb[:, 0:half, :],
                         ctx_rows[0:half * P, :].rearrange("(b p) d -> p b d", p=P)).then_inc(ctx_in, 16)
            for u in range(2):
                sp.dma_start(x_in[:, u, :], x_rows[u * P:(u + 1) * P, :]).then_inc(x_in_done, 16)
            sp.dma_start(ctx_sb[:, half:full, :],
                         ctx_rows[half * P:full * P, :].rearrange("(b p) d -> p b d", p=P)).then_inc(ctx_in, 16)
            sp.dma_start(ctx_sb[0:S_LAST, full, :], ctx_rows[full * P:S, :]).then_inc(ctx_in, 16)
            w_load("v", Wv, wvo_in)
            w_load("o", Wo, wvo_in)
            sp.dma_start(w1_sb[:, :, :], w1.rearrange("(b p) d -> p b d", p=P)).then_inc(wff_in, 16)
            sp.dma_start(w2_sb[:, :, :], w2.rearrange("(c p) f -> p c f", p=P)).then_inc(wff_in, 16)
            for u in range(2):
                sp.dma_start(x_res[:, u, :], x_rows[u * P:(u + 1) * P, :]).then_inc(x_res_in[u], 16)

            def load_x(j):
                for u in range(2):
                    sp.wait_ge(xn_ready, j * 2 + u - 1)
                    sp.dma_start(x_in[:, u, :], x_rows[bass.ds((j * 2 + u) * P, P), :]).then_inc(x_in_done, 16)

            def load_residual(t, u):
                sp.wait_ge(x2_step, (t - 2) * X2S + 2)
                sp.dma_start(x_res[:, u, :], x_rows[bass.ds(t * P, P), :]).then_inc(x_res_in[u], 16)

            load_x(1)

            def do_round(r, stage):
                if stage + 2 < PAIRS:
                    load_x(r + 2)
                if 1 <= stage < PAIRS:
                    load_residual(r * 2 + 1, 1)
                if stage >= 2:
                    for u in range(2):
                        sp.wait_ge(result_taken, taken_out(r - 2, u))
                        sp.dma_start(out_rows[bass.ds(((r - 2) * 2 + u) * P, P), :], o_sb[:, u, :]).then_inc(stored, 16)
                if stage + 1 < PAIRS:
                    load_residual(r * 2 + 2, 0)

            rounds(sp, do_round)
            sp.wait_ge(stored, 16 * TILES)

        @block.gpsimd
        def _(pool):
            pool.memset(ident[:, :], 0.0).then_inc(ident_ready, 1)
            pool.wait_ge(ident_ready, 1)
            pool.affine_select(out=ident[:, :], in_=ident[:, :], compare_op=ALU.not_equal, fill=1.0,
                               base=0, pattern=[[-1, P]], channel_multiplier=1).then_inc(ident_ready, 1)
            pool.memset(minus_half[:, :], -0.5).then_inc(const_ready, 1)
            pool.memset(minus_one[:, :], -1.0).then_inc(const_ready, 1)
            pool.memset(magic_col[:, :], MAGIC).then_inc(const_ready, 1)
            pool.memset(unmagic_col[:, :], -MAGIC).then_inc(const_ready, 1)
            pool.memset(ones[:, :], 1.0).then_inc(const_ready, 1)
            pool.memset(vo[:, :, D:DV], 1.0).then_inc(const_ready, 1)
            pool.dma_start(bk_col[:, :], bk.rearrange("(c p) -> p c", p=P), allow_slow_non_contiguous=True).then_inc(bias_in, 16)
            pool.dma_start(bq_col[:, :], bq.rearrange("(c p) -> p c", p=P), allow_slow_non_contiguous=True).then_inc(bias_in, 16)
            pool.dma_start(bv_col[:, :], bv.rearrange("(c p) -> p c", p=P), allow_slow_non_contiguous=True).then_inc(bias_in, 16)
            pool.dma_start(bo_bc[:, :], bo.partition_broadcast(P)).then_inc(bias_in, 16)
            pool.dma_start(b1_bc[:, :], b1.partition_broadcast(P)).then_inc(bias_in, 16)
            pool.dma_start(b2_bc[:, :], b2.partition_broadcast(P)).then_inc(bias_in, 16)
            pool.wait_ge(const_ready, 6)

            def normalise(j):
                wait_apart(pool, ln1_step, (j + 1) * 4)
                pool.tensor_scalar(ln1_r[:, 0, :], ln1_mv[:, :, 1], EPS, None, ALU.add).then_inc(ln1_row, 1)
                pool.wait_ge(ln1_row, j * 2 + 1)
                pool.tensor_tensor(ln1_r[:, 1, :], ln1_r[:, 0, :], minus_half[:, :], ALU.pow).then_inc(ln1_row, 1)
                wait_apart(pool, ln1_row, j * 2 + 2)
                for u in range(2):
                    pool.tensor_scalar(xn[:, u, :], x_in[:, u, :], ln1_mv[:, u, 0:1], ln1_r[:, 1, u:u + 1],
                                       ALU.subtract, ALU.mult).then_inc(xn_ready, 1)

            def residual(t, u):
                pool.wait_ge(x_res_in[u], (t // 2 + 1) * 16 if isinstance(t, int) else t * 8 + (16 - 8 * u))
                pool.tensor_tensor(x_res[:, u, :], x_res[:, u, :], bo_bc[:, :], ALU.add).then_inc(xb_ready, 1)

            def row_scales_1(j):
                mean_var, base = ln2_mv, j * ROW1
                wait_apart(pool, x2_step, (j + 1) * 2 * X2S)
                n = [0]

                def step(ins):
                    ins.then_inc(row1_step, 1)
                    n[0] += 1
                    wait_apart(pool, row1_step, base + n[0])

                ve, r1, r1s, vn, vne, r2, rr, z, zc, iz, sc, dq = (row1[:, k, :] for k in range(12))
                var = mean_var[:, :, 1]
                step(pool.tensor_scalar(ve, var, EPS, None, ALU.add))
                step(pool.tensor_tensor(r1, ve, minus_half[:, :], ALU.pow))
                step(pool.tensor_tensor(r1s, r1, r1, ALU.mult))
                step(pool.tensor_tensor(vn, r1s, var, ALU.mult))
                step(pool.tensor_scalar(vne, vn, EPS, None, ALU.add))
                step(pool.tensor_tensor(r2, vne, minus_half[:, :], ALU.pow))
                step(pool.tensor_tensor(rr, r1, r2, ALU.mult))
                step(pool.tensor_tensor(z, rr, cen_max[:, :], ALU.mult))
                step(pool.tensor_scalar(zc, z, 1e-5, None, ALU.max))
                step(pool.tensor_tensor(iz, zc, minus_one[:, :], ALU.pow))
                step(pool.tensor_scalar(iz, iz, 127.0, None, ALU.mult))
                step(pool.tensor_tensor(sc, iz, rr, ALU.mult))
                step(pool.tensor_scalar(dq, zc, 1.0 / 127.0, wmean[:, 0:1], ALU.mult, ALU.mult))

            def quantise_1(j):
                for u in range(2):
                    pool.tensor_scalar(y1[:, u, :], cen[:, u, :], row1[:, 10, u:u + 1], MAGIC,
                                       ALU.mult, ALU.add).then_inc(y1_ready, 1)

            def keep_residual(j):
                for u in range(2):
                    pool.tensor_tensor(x2b[:, u, :], x2[:, u, :], b2_bc[:, :], ALU.add).then_inc(x2b_ready, 1)

            def row_scales_2(j):
                base = j * ROW2
                pool.wait_ge(g_sq_ready, (j + 1) * 2)
                wait_apart(pool, g_max_ready, (j + 1) * 2)
                n = [0]

                def step(ins):
                    ins.then_inc(row2_step, 1)
                    n[0] += 1
                    wait_apart(pool, row2_step, base + n[0])

                ms, r, z, zc, iz, iz2, sc, dq = (row2[:, k, :] for k in range(8))
                step(pool.tensor_scalar(ms, g_ssq[:, :], 1.0 / F, EPS, ALU.mult, ALU.add))
                step(pool.tensor_tensor(r, ms, minus_half[:, :], ALU.pow))
                step(pool.tensor_tensor(z, r, g_max[:, :], ALU.mult))
                step(pool.tensor_scalar(zc, z, 1e-5, None, ALU.max))
                step(pool.tensor_tensor(iz, zc, minus_one[:, :], ALU.pow))
                step(pool.tensor_scalar(iz2, iz, 127.0, None, ALU.mult))
                step(pool.tensor_tensor(sc, iz2, r, ALU.mult))
                step(pool.tensor_scalar(dq, zc, 1.0 / 127.0, wmean[:, 1:2], ALU.mult, ALU.mult))

            normalise(0)
            pool.wait_ge(prep_ready, JOB_Q0 + 1)
            normalise(1)
            pool.wait_ge(wscale_step, 2)
            pool.wait_ge(bias_in, 6 * 16)
            pool.wait_ge(prep_taken, PREPS_BVO)
            pool.tensor_tensor(bo_bc[:, :], bo_bc[:, :], bvo_bc[:, :], ALU.add).then_inc(bo_ready, 1)
            pool.wait_ge(bo_ready, 1)
            residual(0, 0)

            def do_round(r, stage):
                if stage + 2 < PAIRS:
                    pool.wait_ge(xn_turned, r + 1)
                    normalise(r + 2)
                if 2 <= stage:
                    row_scales_2(r - 2)
                if 1 <= stage <= PAIRS:
                    row_scales_1(r - 1)
                    quantise_1(r - 1)
                if stage < PAIRS:
                    residual(r * 2 + 1, 1)
                if 1 <= stage <= PAIRS:
                    if stage >= 2:
                        pool.wait_ge(result_taken, taken_out(r - 2, 1))
                    keep_residual(r - 1)
                if stage + 1 < PAIRS:
                    residual(r * 2 + 2, 0)

            rounds(pool, do_round)

        @block.scalar
        def _(act):
            def taken(n, dst, src, **how):
                act.wait_ge(prep_ready, n + 1)
                act.activation(dst, src, ACT.Identity, **how).then_inc(prep_taken, 1)

            def bank(n):
                return prep[n % 4]

            def copy_scores(t, u, c):
                at, n = CHUNKS[c]
                act.wait_ge(s_ready, t * SC + c + 1)
                act.activation(s_sb[:, u, at:at + n], score[c][:, 0:n], ACT.Copy).then_inc(s_copied, 1)

            act.wait_ge(const_ready, 6)
            for k, n in enumerate("kq"):
                taken(JOB_WQK + k, WT[n][:, :, :], bank(JOB_WQK + k)[:, :].rearrange("p (c o) -> p c o", c=DC))
            for k in range(NCTX):
                n = min(2 * P, S - 2 * k * P)
                src = bank(JOB_CTX + k)[:, :].rearrange("p (c s) -> p c s", c=DC)[:, :, 0:n]
                taken(JOB_CTX + k, ctxT[:, :, 2 * k * P:2 * k * P + n], src)
            act.wait_ge(bias_in, 6 * 16)
            for k in range(SC * DC):
                (at, n), o = CHUNKS[k // DC], k % DC
                taken(JOB_K + k, kT[:, o, at:at + n], bank(JOB_K + k)[:, 0:n], bias=bk_col[:, o:o + 1])
            taken(JOB_Q0, xnT[:, :, :], bank(JOB_Q0)[:, :].rearrange("p (c t) -> p c t", c=DC))
            act.wait_ge(prep_ready, JOB_Q0 + 2)
            for o in range(DC):
                act.activation(qT[:, o, :], bank(JOB_Q0 + 1)[:, o * 2 * P:(o + 1) * 2 * P], ACT.Identity,
                               bias=bq_col[:, o:o + 1]).then_inc(q_ready, 1)
            for c in range(SC):
                copy_scores(0, 0, c)
            for c in range(SC):
                copy_scores(1, 1, c)
            taken(JOB_WO, WT["o"][:, :, :], bank(JOB_WO)[:, :].rearrange("p (c o) -> p c o", c=DC))
            taken(JOB_WVO, wvoT[:, :, :], bank(JOB_WVO)[:, :].rearrange("p (c o) -> p c o", c=DC))
            taken(JOB_BVO, bvo_bc[:, :], bank(JOB_BVO)[:, 0:D])
            for k in range(NCTX):
                nb = min(2, SB - 2 * k)
                rows = P if 2 * k + nb < SB else S_LAST
                taken(JOB_VO + k, vo[0:rows, 2 * k:2 * k + nb, 0:D],
                      bank(JOB_VO + k)[0:rows, 0:nb * D].rearrange("p (b d) -> p b d", b=nb))
            for k in range(4):
                b = k % 2 * 4
                taken(JOB_W1 + k, w1T[:, k // 2, b * P:(b + 4) * P], bank(JOB_W1 + k)[:, :], bias=unmagic_col[:, 0:1])
            for k in range(4):
                c, b = k // 2, k % 2 * 4
                taken(JOB_W2 + k, w2T[:, b:b + 4, c * P:(c + 1) * P],
                      bank(JOB_W2 + k)[:, :].rearrange("p (b o) -> p b o", b=4), bias=unmagic_col[:, 0:1])

            turns = Count(TURNS)

            def take_turn(dst, cols, parts=1, bias=None):
                k = turns.before % 2
                act.wait_ge(turned, turns.next() + 1)
                src = turn[k][0:dst.shape[0], 0:cols]
                if parts > 1:
                    src = src.rearrange("p (b n) -> p b n", b=parts)
                if bias is None:
                    act.activation(dst, src, ACT.Copy).then_inc(turn_taken, 1)
                else:
                    act.activation(dst, src, ACT.Identity, bias=bias).then_inc(turn_taken, 1)

            def take_weights(q):
                lo, hi = QUADS[q]
                rows = P if hi < SB else S_LAST
                take_turn(pT[0:rows, lo * P:hi * P], (hi - lo) * P)

            def exp_all(t, u):
                act.wait_ge(max_ready, t + 1)
                act.activation(e_all[:, u, :], s_sb[:, u, :], ACT.Exp, bias=neg_max[:, u:u + 1],
                               scale=SCALE).then_inc(e_ready, 1)

            def do_round(r, stage):
                if 1 <= stage < PAIRS:
                    act.wait_ge(p_ready, r * 2)
                    for c in range(SC):
                        copy_scores(r * 2 + 1, 1, c)
                if stage < PAIRS:
                    exp_all(r * 2, 0)
                if 1 <= stage <= PAIRS:
                    take_weights(0)
                    take_weights(1)
                if stage + 1 < PAIRS:
                    take_turn(xnT[:, :, :], 2 * D, DC)
                if 1 <= stage <= PAIRS:
                    take_weights(2)
                if stage + 1 < PAIRS:
                    for o in range(DC):
                        take_turn(qT[:, o, :], 2 * P, 1, bq_col[:, o:o + 1])
                if 1 <= stage <= PAIRS:
                    take_weights(3)
                if stage >= 2:
                    for u in range(2):
                        act.wait_ge(result_taken, taken_h(r - 2, u))
                        act.activation(g[:, u, :], g[:, u, :], ACT.Gelu).then_inc(g_ready, 1)
                    for u in range(2):
                        act.wait_ge(g_ready, (r - 2) * 2 + u + 1)
                        if u or stage >= 3:
                            act.wait_ge(g_sq_ready, (r - 2) * 2 + u)
                        act.activation(g_sq[:, :], g[:, u, :], ACT.Square,
                                       accum_out=g_ssq[:, u:u + 1]).then_inc(g_sq_ready, 1)
                if stage + 1 < PAIRS:
                    act.wait_ge(p_ready, r * 2 + 1)
                    for c in range(SC):
                        copy_scores(r * 2 + 2, 0, c)
                if stage < PAIRS:
                    exp_all(r * 2 + 1, 1)
                    for q in range(NT):
                        take_weights(q)
                if stage >= 2:
                    act.wait_ge(row2_step, (r - 1) * ROW2)
                    for u in range(2):
                        act.activation(y2[:, u, :], g[:, u, :], ACT.Identity, scale=row2[:, 6, u:u + 1],
                                       bias=magic_col[:, 0:1]).then_inc(y2_ready, 1)
                    for u in range(2):
                        for h in range(2):
                            take_turn(y2T[:, h * 4:h * 4 + 4, u * P:(u + 1) * P], BANK, 4, unmagic_col[:, 0:1])
                if 1 <= stage <= PAIRS:
                    take_turn(y1T[:, :, :], 2 * D, DC, unmagic_col[:, 0:1])

            rounds(act, do_round, [turns])

        @block.vector
        def _(dve):
            def ln1_part_stats(j):
                dve.wait_ge(x_in_done, (j + 1) * 32)
                for u in range(2):
                    dve.bn_stats(ln1_part[:, u, :], x_in[:, u, :]).then_inc(ln1_step, 1)

            def ln1_stats(j):
                for u in range(2):
                    wait_apart(dve, ln1_step, j * 4 + u + 1)
                    dve.bn_aggr(ln1_mv[:, u, :], ln1_part[:, u, :]).then_inc(ln1_step, 1)

            def candidates(t, u):
                wait_apart(dve, s_copied, (t + 1) * SC)
                for k in range(PIECES):
                    end = (k + 1) * PIECE if k < PIECES - 1 else S
                    ins = dve.max(cand[:, u, 8 * k:8 * k + 8], s_sb[:, u, k * PIECE:end])
                ins.then_inc(cand_ready, 1)

            TOPK_STEPS = 2 * ROUNDS - 1

            def best_8(t, u, k):
                if k == 0:
                    wait_apart(dve, cand_ready, t + 1)
                else:
                    wait_apart(dve, topk_step, t * TOPK_STEPS + 2 * k)
                dve.max(best[:, k, :], cand_left[:, :] if k else cand[:, u, :]).then_inc(topk_step, 1)
                if k == 0:
                    dve.wait_ge(topk_step, t * TOPK_STEPS + 1)
                    dve.tensor_scalar(neg_max[:, u:u + 1], best[:, 0, 0:1], -SCALE, None,
                                      ALU.mult).then_inc(max_ready, 1)

            def drop_8(t, u, k):
                wait_apart(dve, topk_step, t * TOPK_STEPS + 2 * k + 1)
                dve.match_replace(cand_left[:, :], best[:, k, :], cand_left[:, :] if k else cand[:, u, :],
                                  LOWEST).then_inc(topk_step, 1)

            SETTLE_STEPS = 8

            def settled(t, n):
                dve.wait_ge(settle_step, t * SETTLE_STEPS + n)

            def count_kept(t, u):
                least = best[:, ROUNDS - 1, 7:8]
                dve.wait_ge(topk_step, (t + 1) * TOPK_STEPS)
                dve.tensor_scalar(cand_ge[:, :], cand[:, u, :], least, 0.0, ALU.is_ge, ALU.add,
                                  accum_out=counts[:, 0:1]).then_inc(settle_step, 1)
                dve.wait_ge(settle_step, t * SETTLE_STEPS + 1)
                dve.tensor_scalar(cand_ge[:, 0:PIECES], cand[:, u, 7:CAND:8], least, 0.0, ALU.is_ge, ALU.add,
                                  accum_out=counts[:, 1:2]).then_inc(settle_step, 1)

            def doubts(t):
                settled(t, 2)
                dve.scalar_tensor_tensor(doubt[:, 0:1], counts[:, 0:1], float(TOPK), counts[:, 1:2], ALU.subtract,
                                         ALU.add).then_inc(settle_step, 1)

            def doubts_in_row(t):
                settled(t, 3)
                dve.transpose(doubt_row[:, 0:32], doubt[:, :]).then_inc(settle_step, 1)

            def gather_doubts(t):
                settled(t, 4)
                for k in range(1, 4):
                    dve.tensor_copy(doubt_row[0:1, 32 * k:32 * k + 32],
                                    doubt_row[32 * k:32 * k + 1, 0:32]).then_inc(settle_step, 1)

            def largest_doubt(t, u):
                settled(t, 7)
                dve.tensor_reduce(doubtful[:, u:u + 1], doubt_row[0:1, :], AX.X, ALU.max).then_inc(settle_step, 1)

            def weigh(t, u):
                dve.wait_ge(e_ready, t + 1)
                dve.scalar_tensor_tensor(e_all[:, u, :], s_sb[:, u, :], best[:, ROUNDS - 1, 7:8], e_all[:, u, :],
                                         ALU.is_ge, ALU.mult).then_inc(masked, 1)
                wait_apart(dve, settle_step, (t + 1) * SETTLE_STEPS)
                left = dve.value_load(doubtful[0:1, u:u + 1], min_val=0, max_val=2 * CAND)
                with dve.If(left > 0):
                    dve.sem_clear(general_step)
                    for k in range(ROUNDS):
                        src = s_left[:, :] if k else s_sb[:, u, :]
                        if k:
                            dve.wait_ge(general_step, 2 * k)
                        dve.max(best_of_all[:, :], src).then_inc(general_step, 1)
                        dve.wait_ge(general_step, 2 * k + 1)
                        dve.match_replace(s_left[:, :], best_of_all[:, :], src, LOWEST).then_inc(general_step, 1)
                    dve.wait_ge(general_step, 2 * ROUNDS)
                    dve.wait_ge(masked, t + 1)
                    dve.scalar_tensor_tensor(e_all[:, u, :], s_left[:, :], LOWEST, e_all[:, u, :], ALU.is_equal,
                                             ALU.mult).then_inc(general_step, 1)
                    dve.wait_ge(general_step, 2 * ROUNDS + 1)
                with dve.Else():
                    pass
                dve.wait_ge(masked, t + 1)
                dve.sem_inc(p_ready, 1)

            results = Count(RESULTS)

            def take_result():
                k, n = results.before % 2, results.next() + 1
                dve.wait_ge(result_ready, n)
                return result[k], n

            def attended(t, u, n):
                base = t * X2S
                if n == 0:
                    x2_bank[0], x2_bank[1] = take_result()
                    dve.wait_ge(xb_ready, t + 1)
                    dve.reciprocal(inv_sum[:, u:u + 1], x2_bank[0][:, D:DV]).then_inc(x2_step, 1)
                if n == 1:
                    if not isinstance(t, int) or t >= 2:
                        dve.wait_ge(x2b_ready, t - u)
                    dve.wait_ge(x2_step, base + 1)
                    dve.scalar_tensor_tensor(x2[:, u, :], x2_bank[0][:, 0:D], inv_sum[:, u:u + 1], x_res[:, u, :],
                                             ALU.mult, ALU.add).then_inc(result_taken, 1)
                if n == 2:
                    dve.wait_ge(result_taken, x2_bank[1])
                    dve.bn_stats(ln2_part[:, u, :], x2[:, u, :]).then_inc(x2_step, 1)
                if n == 3:
                    wait_apart(dve, x2_step, base + 2)
                    dve.bn_aggr(ln2_mv[:, u, :], ln2_part[:, u, :]).then_inc(x2_step, 1)
                if n == 4:
                    dve.wait_ge(x2_step, base + 3)
                    dve.tensor_scalar(cen[:, u, :], x2[:, u, :], ln2_mv[:, u, 0:1], None,
                                      ALU.subtract).then_inc(x2_step, 1)
                if n == 5:
                    dve.wait_ge(x2_step, base + 4)
                    dve.tensor_reduce(cen_max[:, u:u + 1], cen[:, u, :], AX.X, ALU.max,
                                      apply_absolute_value=True).then_inc(x2_step, 1)

            x2_bank = [None, None]

            def hidden(j):
                dve.wait_ge(row1_step, (j + 1) * ROW1)
                for u in range(2):
                    for h in range(2):
                        bank, _ = take_result()
                        dve.scalar_tensor_tensor(g[:, u, h * BANK:(h + 1) * BANK], bank[:, :], row1[:, 11, u:u + 1],
                                                 b1_bc[:, h * BANK:(h + 1) * BANK], ALU.mult,
                                                 ALU.add).then_inc(result_taken, 1)

            def gelu_max(j, u):
                dve.wait_ge(g_ready, j * 2 + u + 1)
                dve.tensor_reduce(g_max[:, u:u + 1], g[:, u, :], AX.X, ALU.max,
                                  apply_absolute_value=True).then_inc(g_max_ready, 1)

            def output(j, u):
                dve.wait_ge(x2b_ready, (j + 1) * 2)
                if not isinstance(j, int) or j > 0:
                    dve.wait_ge(stored, j * 32)
                bank, _ = take_result()
                dve.scalar_tensor_tensor(o_sb[:, u, :], bank[:, 0:D], row2[:, 7, u:u + 1],
                                         x2b[:, u, :], ALU.mult, ALU.add).then_inc(result_taken, 1)

            dve.memset(doubt[:, :], 0.0).then_inc(doubt_cleared, 1)
            dve.wait_ge(doubt_cleared, 1)
            for j in range(2):
                ln1_part_stats(j)
                ln1_stats(j)
            dve.wait_ge(const_ready, 6)
            dve.wait_ge(bias_in, 6 * 16)
            for c in range(DC):
                dve.tensor_scalar(bv_bc[:, c, :], ones[:, :], bv_col[:, c:c + 1], None, ALU.mult).then_inc(bv_spread, 1)
            dve.wait_ge(wff_in, 32)
            for k, w in enumerate((w1_sb, w2_sb)):
                dve.tensor_reduce(wsum[:, k:k + 1], w[:, :, :], AX.XY, ALU.add,
                                  apply_absolute_value=True).then_inc(wsum_ready, 1)
            dve.wait_ge(prep_ready, JOB_MEAN + 1)
            dve.tensor_scalar(wmean[:, :], prep[JOB_MEAN % 4][:, 0:2], 1.0 / (D * F), 1e-5,
                              ALU.mult, ALU.max).then_inc(wscale_step, 1)
            dve.wait_ge(wscale_step, 1)
            dve.reciprocal(winv[:, :], wmean[:, :]).then_inc(wscale_step, 1)
            dve.wait_ge(wscale_step, 2)
            for k, w in enumerate((w1_sb, w2_sb)):
                dve.tensor_scalar(w[:, :, :], w[:, :, :], winv[:, k:k + 1], MAGIC, ALU.mult,
                                  ALU.add).then_inc(wscale_step, 1)
                dve.wait_ge(wscale_step, 3 + k)
                dve.tensor_scalar(w[:, :, :], w[:, :, :], MAGIC + 1.0, MAGIC - 1.0, ALU.min,
                                  ALU.max).then_inc(ternary_ready, 1)

            candidates(0, 0)

            def do_round(r, stage):
                attention, x2_now, late = stage < PAIRS, 1 <= stage <= PAIRS, 2 <= stage
                if attention:
                    best_8(r * 2, 0, 0)
                if stage + 2 < PAIRS:
                    ln1_part_stats(r + 2)
                if attention:
                    drop_8(r * 2, 0, 0)
                if stage + 2 < PAIRS:
                    ln1_stats(r + 2)
                if attention:
                    best_8(r * 2, 0, 1)
                    drop_8(r * 2, 0, 1)
                    best_8(r * 2, 0, 2)
                    drop_8(r * 2, 0, 2)
                    best_8(r * 2, 0, 3)
                    count_kept(r * 2, 0)
                    doubts(r * 2)
                    doubts_in_row(r * 2)
                    gather_doubts(r * 2)
                    largest_doubt(r * 2, 0)
                    weigh(r * 2, 0)
                    candidates(r * 2 + 1, 1)
                if late:
                    gelu_max(r - 2, 0)
                    gelu_max(r - 2, 1)
                if x2_now:
                    attended(r * 2 - 1, 1, 0)
                if attention:
                    best_8(r * 2 + 1, 1, 0)
                if x2_now:
                    attended(r * 2 - 1, 1, 1)
                if attention:
                    drop_8(r * 2 + 1, 1, 0)
                if x2_now:
                    attended(r * 2 - 1, 1, 2)
                if attention:
                    best_8(r * 2 + 1, 1, 1)
                if x2_now:
                    attended(r * 2 - 1, 1, 3)
                if attention:
                    drop_8(r * 2 + 1, 1, 1)
                if x2_now:
                    attended(r * 2 - 1, 1, 4)
                if attention:
                    best_8(r * 2 + 1, 1, 2)
                if x2_now:
                    attended(r * 2 - 1, 1, 5)
                if attention:
                    drop_8(r * 2 + 1, 1, 2)
                if attention:
                    best_8(r * 2 + 1, 1, 3)
                    count_kept(r * 2 + 1, 1)
                    doubts(r * 2 + 1)
                    doubts_in_row(r * 2 + 1)
                    gather_doubts(r * 2 + 1)
                    largest_doubt(r * 2 + 1, 1)
                    weigh(r * 2 + 1, 1)
                if stage + 1 < PAIRS:
                    candidates(r * 2 + 2, 0)
                if late:
                    output(r - 2, 0)
                    output(r - 2, 1)
                if attention:
                    for n in range(6):
                        attended(r * 2, 0, n)
                if x2_now:
                    hidden(r - 1)

            rounds(dve, do_round, [results])

        @block.tensor
        def _(pe):
            def prep_bank(n):
                if n >= 4:
                    pe.wait_ge(prep_taken, taken_before(n - 3))
                if n - 4 == JOB_MEAN:
                    pe.wait_ge(wscale_step, 1)
                return prep[n % 4]

            def taken_before(n):
                return n - (n > JOB_Q0 + 1) - (n > JOB_MEAN)

            def prep_turn(n, blocks):
                bank = prep_bank(n)
                for k, (src, at) in enumerate(blocks):
                    rows = src.shape[0]
                    ins = pe.transpose(bank[:, at:at + rows], src, ident[0:rows, 0:rows])
                ins.then_inc(prep_ready, 1)

            def weights_T(n, name):
                prep_turn(n, [(W4[name][:, o, c * P:(c + 1) * P], c * D + o * P) for c in range(DC) for o in range(DC)])

            def project(n0, w):
                for k in range(SC * DC):
                    (at, n), o = CHUNKS[k // DC], k % DC
                    bank = prep_bank(n0 + k)
                    for c in range(DC):
                        ins = pe.matmul(bank[:, 0:n], WT[w][:, c, o * P:(o + 1) * P], ctxT[:, c, at:at + n],
                                        start=(c == 0), stop=(c == DC - 1))
                    ins.then_inc(prep_ready, 1)

            def scores(t, u, c):
                at, n = CHUNKS[c]
                if u or not isinstance(t, int) or t > 0:
                    pe.wait_ge(s_copied, (t - 1) * SC + c + 1)
                for k in range(DC):
                    ins = pe.matmul(score[c][:, 0:n], qT[:, k, u * P:(u + 1) * P], kT[:, k, at:at + n],
                                    start=(k == 0), stop=(k == DC - 1))
                ins.then_inc(s_ready, 1)

            pe.wait_ge(ident_ready, 2)
            pe.wait_ge(wqk_in, 32)
            weights_T(JOB_WQK, "k")
            weights_T(JOB_WQK + 1, "q")
            for k in range(NCTX):
                if k == 0:
                    pe.wait_ge(ctx_in, 48)
                blocks = []
                for b in range(2 * k, min(2 * k + 2, SB)):
                    rows = P if b < SB - 1 else S_LAST
                    blocks += [(ctx_sb[0:rows, b, c * P:(c + 1) * P], c * D + (b - 2 * k) * P) for c in range(DC)]
                prep_turn(JOB_CTX + k, blocks)
            pe.wait_ge(prep_taken, JOB_K)
            project(JOB_K, "k")
            pe.wait_ge(wsum_ready, 2)
            pe.wait_ge(const_ready, 6)
            pe.matmul(prep_bank(JOB_MEAN)[:, 0:2], ones[:, :], wsum[:, :], start=True, stop=True).then_inc(prep_ready, 1)
            pe.wait_ge(xn_ready, 2)
            prep_turn(JOB_Q0, [(xn[:, u, c * P:(c + 1) * P], c * D + u * P) for c in range(DC) for u in range(2)])
            bank = prep_bank(JOB_Q0 + 1)
            pe.wait_ge(prep_taken, taken_before(JOB_Q0 + 1))
            for o in range(DC):
                for c in range(DC):
                    ins = pe.matmul(bank[:, o * 2 * P:(o + 1) * 2 * P], WT["q"][:, c, o * P:(o + 1) * P], xnT[:, c, :],
                                    start=(c == 0), stop=(c == DC - 1))
            ins.then_inc(prep_ready, 1)
            pe.wait_ge(q_ready, DC)
            for c in range(SC):
                scores(0, 0, c)
            for c in range(SC):
                scores(1, 1, c)
            pe.wait_ge(wvo_in, 32)
            weights_T(JOB_WO, "o")
            pe.wait_ge(prep_taken, taken_before(JOB_WO + 1))
            bank = prep_bank(JOB_WVO)
            for i in range(DC):
                for c in range(DC):
                    ins = pe.matmul(bank[:, i * D:(i + 1) * D], W4["v"][:, c, i * P:(i + 1) * P], WT["o"][:, c, :],
                                    start=(c == 0), stop=(c == DC - 1))
            ins.then_inc(prep_ready, 1)
            bank = prep_bank(JOB_BVO)
            pe.wait_ge(bv_spread, DC)
            for c in range(DC):
                ins = pe.matmul(bank[:, 0:D], bv_bc[:, c, :], WT["o"][:, c, :], start=(c == 0), stop=(c == DC - 1))
            ins.then_inc(prep_ready, 1)
            pe.wait_ge(prep_taken, taken_before(JOB_WVO + 1))
            for k in range(NCTX):
                bank = prep_bank(JOB_VO + k)
                for b in range(2 * k, min(2 * k + 2, SB)):
                    rows = P if b < SB - 1 else S_LAST
                    at = (b - 2 * k) * D
                    for c in range(DC):
                        ins = pe.matmul(bank[0:rows, at:at + D], ctxT[:, c, b * P:b * P + rows], wvoT[:, c, :],
                                        start=(c == 0), stop=(c == DC - 1))
                ins.then_inc(prep_ready, 1)
            pe.wait_ge(ternary_ready, 1)
            for k in range(4):
                c, b = k // 2, k % 2 * 4
                prep_turn(JOB_W1 + k, [(w1_sb[:, b + i, c * P:(c + 1) * P], i * P) for i in range(4)])
            pe.wait_ge(ternary_ready, 2)
            for k in range(4):
                c, b = k // 2, k % 2 * 4
                prep_turn(JOB_W2 + k, [(w2_sb[:, c, (b + i) * P:(b + i + 1) * P], i * P) for i in range(4)])
            pe.wait_ge(prep_taken, taken_before(PREPS))

            turns, results = Count(TURNS), Count(RESULTS)

            def turn_bank():
                k, first = turns.before % 2, turns.loop is None and turns.before < 2
                n = turns.next()
                if not first:
                    pe.wait_ge(turn_taken, n - 1)
                return turn[k]

            def result_bank():
                k, first = results.before % 2, results.loop is None and results.before < 2
                n = results.next()
                if not first:
                    pe.wait_ge(result_taken, n - 1)
                return result[k]

            def turn_weights(u, q):
                bank = turn_bank()
                lo, hi = QUADS[q]
                for b in range(lo, hi):
                    n = P if b < SB - 1 else S_LAST
                    ins = pe.transpose(bank[0:n, (b - lo) * P:(b - lo + 1) * P],
                                       e_all[:, u, b * P:b * P + n], ident[:, :])
                ins.then_inc(turned, 1)

            def weighted(bank, q, landed):
                pe.wait_ge(turn_taken, landed)
                lo, hi = QUADS[q]
                for b in range(lo, hi):
                    n = P if b < SB - 1 else S_LAST
                    ins = pe.matmul(bank[:, 0:DV], pT[0:n, b * P:(b + 1) * P], vo[0:n, b, :],
                                    start=(b == 0), stop=(b == SB - 1))
                return ins

            def turn_y2(u, h):
                bank = turn_bank()
                for k in range(4):
                    ins = pe.transpose(bank[:, k * P:(k + 1) * P], y2[:, u, (h * 4 + k) * P:(h * 4 + k + 1) * P],
                                       ident[:, :])
                ins.then_inc(turned, 1)

            def turn_pair(src):
                bank = turn_bank()
                for c in range(DC):
                    for u in range(2):
                        ins = pe.transpose(bank[:, c * D + u * P:c * D + (u + 1) * P], src[:, u, c * P:(c + 1) * P],
                                           ident[:, :])
                ins.then_inc(turned, 1)

            def turned_so_far():
                n = turns.before
                return n if turns.loop is None else (turns.loop - LOOP[0]) * TURNS + n

            def sum_weighted(landed):
                bank = result_bank()
                for q in range(NT):
                    ins = weighted(bank, q, landed[q])
                ins.then_inc(result_ready, 1)

            def do_round(r, stage):
                more, before, late = stage + 1 < PAIRS, 1 <= stage <= PAIRS, stage >= 2
                landed = [None] * NT
                if before:
                    pe.wait_ge(p_ready, r * 2)
                    for q in range(2):
                        turn_weights(1, q)
                        landed[q] = turned_so_far()
                if more:
                    pe.wait_ge(xn_ready, (r + 2) * 2)
                    turn_pair(xn)
                    xn_landed = turned_so_far()
                if before:
                    turn_weights(1, 2)
                    landed[2] = turned_so_far()
                if more:
                    for o in range(DC):
                        bank = turn_bank()
                        if o == 0:
                            pe.wait_ge(turn_taken, xn_landed)
                            pe.sem_inc(xn_turned, 1)
                        for c in range(DC):
                            ins = pe.matmul(bank[:, 0:2 * P], WT["q"][:, c, o * P:(o + 1) * P],
                                            xnT[:, c, :], start=(c == 0), stop=(c == DC - 1))
                        ins.then_inc(turned, 1)
                    queries_landed = turned_so_far()
                if before:
                    turn_weights(1, 3)
                    landed[3] = turned_so_far()
                    sum_weighted(landed)
                if more:
                    pe.wait_ge(turn_taken, queries_landed)
                    for c in range(SC):
                        scores(r * 2 + 2, 0, c)
                if stage < PAIRS:
                    pe.wait_ge(p_ready, r * 2 + 1)
                    for q in range(NT):
                        turn_weights(0, q)
                        landed[q] = turned_so_far()
                        if more and q % 2:
                            scores(r * 2 + 3, 1, q // 2)
                if late:
                    for u in range(2):
                        pe.wait_ge(y2_ready, (r - 2) * 2 + u + 1)
                        for h in range(2):
                            turn_y2(u, h)
                    for u in range(2):
                        bank = result_bank()
                        pe.wait_ge(turn_taken, turned_so_far() - 2 + 2 * u)
                        for b in range(FB):
                            ins = pe.matmul(bank[:, 0:D], y2T[:, b, u * P:(u + 1) * P], w2T[:, b, :],
                                            start=(b == 0), stop=(b == FB - 1))
                        ins.then_inc(result_ready, 1)
                if stage < PAIRS:
                    sum_weighted(landed)
                if more:
                    for c in range(NT // 2, SC):
                        scores(r * 2 + 3, 1, c)
                if before:
                    pe.wait_ge(y1_ready, r * 2)
                    turn_pair(y1)
                    y1_landed = turned_so_far()
                    for u in range(2):
                        for h in range(2):
                            bank = result_bank()
                            if u == h == 0:
                                pe.wait_ge(turn_taken, y1_landed)
                            for c in range(DC):
                                ins = pe.matmul(bank[:, :], y1T[:, c, u * P:(u + 1) * P],
                                                w1T[:, c, h * BANK:(h + 1) * BANK], start=(c == 0), stop=(c == DC - 1))
                            ins.then_inc(result_ready, 1)

            rounds(pe, do_round, [turns, results])


_INS = ["x", "ctx_1024", "L0_xattn_Wq", "L0_xattn_bq", "L0_xattn_Wk", "L0_xattn_bk", "L0_xattn_Wv", "L0_xattn_bv",
        "L0_xattn_Wo", "L0_xattn_bo", "L0_ffn_w1", "L0_ffn_b1", "L0_ffn_w2", "L0_ffn_b2"]


def kernel(**inputs):
    from concourse import bacc
    from concourse.bass_utils import run_bass_kernel_spmd

    nc = bacc.Bacc("TRN2", target_bir_lowering=False, num_devices=1)
    arrays, args = {}, []
    for name in _INS:
        a = np.ascontiguousarray(inputs[name])
        arrays[f"in_{name}"] = a
        args.append(nc.dram_tensor(f"in_{name}", a.shape, mybir.dt.from_np(a.dtype), kind="ExternalInput").ap())
    args.append(nc.dram_tensor("out", (1, T, D), F32, kind="ExternalOutput").ap())
    build(nc, *args)
    r = run_bass_kernel_spmd(nc, [arrays], core_ids=[0])
    return r.results[0]["out"]
```

```python
from contextlib import ExitStack

import numpy as np

import concourse.bass as bass
from concourse import mybir

F32 = mybir.dt.float32
BF16 = mybir.dt.bfloat16
F32R = mybir.dt.float32r
ALU = mybir.AluOpType
ACT = mybir.ActivationFunctionType
AX = mybir.AxisListType

P = 128
D = 256
DC = D // P
T = 2048
S = 1601
F = 1024
FB = F // P
BANK = 512
TOPK = 32
ROUNDS = TOPK // 8
TILES = T // P
PAIRS = TILES // 2
SB = -(-S // P)
S_LAST = S - (SB - 1) * P
SC = -(-S // BANK)
S_EVEN = S + S % 2
CHUNKS = [(c * BANK, min(BANK, S - c * BANK)) for c in range(SC)]
CHUNKS.insert(SC - 2, CHUNKS.pop())
QUADS = [(g, min(g + 4, SB)) for g in range(0, SB, 4)]
NT = len(QUADS)
DV = D + 1
SCALE = float(D) ** -0.5
EPS = 1e-5
LOWEST = -3.4028234e38
MAGIC = 12582912.0
PIECE = 50
PIECES = S // PIECE
CAND = 8 * PIECES

TURNS = 1 + 2 + NT + 4 + 1 + NT
RESULTS = 1 + 1 + 2 + 4
ROW1, ROW2, X2S = 7, 7, 5
LOOP = (2, PAIRS - 2)
LAST_ROUND = PAIRS + 2


class Count:

    def __init__(self, per_round):
        self.per_round, self.before, self.loop = per_round, 0, None

    def next(self):
        n = self.before
        self.before += 1
        return n if self.loop is None else (self.loop - LOOP[0]) * self.per_round + n

    def enter(self, register):
        self.loop, self.entry = register, self.before

    def leave(self):
        assert self.before == self.entry + self.per_round
        self.loop = None
        self.before = self.entry + self.per_round * (LOOP[1] - LOOP[0])


def rounds(engine, do_round, counts=()):
    for r in range(LOOP[0]):
        do_round(r, r)
    with engine.Fori(LOOP[0], LOOP[1]) as r:
        for c in counts:
            c.enter(r)
        do_round(r, LOOP[0])
        for c in counts:
            c.leave()
    for r in range(LOOP[1], LAST_ROUND):
        do_round(r, r)


def build(nc, x, ctx, Wq, bq, Wk, bk, Wv, bv, Wo, bo, w1, b1, w2, b2, out):
    x_rows = x.rearrange("a t d -> (a t) d")
    out_rows = out.rearrange("a t d -> (a t) d")
    ctx_rows = ctx.rearrange("a s d -> (a s) d")

    with ExitStack() as stack:
        def sb(name, shape, dt=F32):
            return stack.enter_context(nc.sbuf_tensor(name, shape, dt))

        def sem(name):
            return stack.enter_context(nc.semaphore(name))

        score = [stack.enter_context(nc.psum_tensor(f"score{c}", [P, BANK], F32)) for c in range(SC)]
        turn = [stack.enter_context(nc.psum_tensor(f"turn{c}", [P, BANK], F32)) for c in range(2)]
        result = [stack.enter_context(nc.psum_tensor(f"result{c}", [P, BANK], F32)) for c in range(2)]
        prep = turn + result

        with ExitStack() as early:
            def early_sb(name, shape, dt=F32):
                return early.enter_context(nc.sbuf_tensor(name, shape, dt))

            w1_sb = early_sb("w1_sb", [P, FB, D])
            w2_sb = early_sb("w2_sb", [P, DC, F])
            W_rows = {n: early_sb(f"w_{n}", [P, DC, D]) for n in "qkvo"}
            ctx_high = early_sb("ctx_high", [P, DC, S_EVEN], F32R)
        y2 = sb("y2", [P, 2, F])
        g_usual = sb("g", [P, 2, F])
        g_last = sb("g_last", [P, 2, F])
        y1, o_sb, x2_kept, x2b = (sb(n, [P, 2, D]) for n in ("y1", "o_sb", "x2_kept", "x2b"))
        y2T = sb("y2T", [P, FB, 2 * P], BF16)
        y1T = sb("y1T", [P, DC, 2 * P], BF16)

        def g_of(j):
            return g_last if isinstance(j, int) and j == PAIRS - 1 else g_usual

        WT = {n: sb(f"wt_{n}", [P, DC, D]) for n in "qo"}
        wk_high, wk_low = (sb(n, [P, DC, D], F32R) for n in ("wk_high", "wk_low"))
        wvo_high, wvo_low = (sb(n, [P, DC, D], F32R) for n in ("wvo_high", "wvo_low"))
        bv_bc = sb("bv_bc", [P, DC, P])
        w1T = sb("w1T", [P, DC, F], BF16)
        w2T = sb("w2T", [P, FB, D], BF16)
        bq_col, bk_col, bv_col = (sb(n, [P, DC]) for n in ("bq_col", "bk_col", "bv_col"))
        bo_bc = sb("bo_bc", [P, D])
        bvo_bc = sb("bvo_bc", [P, D])
        b1_bc = sb("b1_bc", [P, F])
        b2_bc = sb("b2_bc", [P, D])
        ident = sb("ident", [P, P])
        ones = sb("ones", [P, P])
        wsum = sb("wsum", [P, 2])
        wmean = sb("wmean", [P, 2])
        winv = sb("winv", [P, 2])
        minus_half = sb("minus_half", [P, 2])
        minus_one = sb("minus_one", [P, 2])
        magic_col = sb("magic_col", [P, 1])
        unmagic_col = sb("unmagic_col", [P, 1])

        ctx_low = sb("ctx_low", [P, DC, S_EVEN], F32R)
        k_high = sb("k_high", [P, DC, S_EVEN], F32R)
        with nc.sbuf_tensor("ctx_sb", [P, SB, D], F32) as ctx_sb:
            pass
        k_low = sb("k_low", [P, SB * D], F32R)[:, 0:DC * S_EVEN].rearrange("p (c s) -> p c s", c=DC)
        vo = sb("vo", [P, SB, DV])

        x_in = sb("x_in", [P, 2, D])
        ln1_part = sb("ln1_part", [P, 2, 6])
        ln1_mv = sb("ln1_mv", [P, 2, 2])
        ln1_r = sb("ln1_r", [P, 2, 2])
        xn = sb("xn", [P, 2, D])
        xnT = sb("xnT", [P, DC, 2 * P])
        q_full = sb("q_full", [P, DC, 2 * P])
        q_high = sb("q_high", [P, DC, 2 * P], F32R)
        q_low = sb("q_low", [P, DC, 2 * P], F32R)

        s_sb = sb("s_sb", [P, 2, S])
        cand = sb("cand", [P, 2, CAND])
        cand_left = sb("cand_left", [P, CAND])
        cand_ge = sb("cand_ge", [P, CAND], BF16)
        best = sb("best", [P, ROUNDS, 8])
        counts = sb("counts", [P, 2])
        doubt = sb("doubt", [P, 32])
        doubt_row = sb("doubt_row", [P, P])
        doubtful = sb("doubtful", [1, 2], mybir.dt.int32)
        s_left = sb("s_left", [P, S])
        best_of_all = sb("best_of_all", [P, 8])
        neg_max = sb("neg_max", [P, 2])
        e_all = sb("e_all", [P, 2, S])
        pT = sb("pT", [P, SB * P])
        inv_sum = sb("inv_sum", [P, 2])
        x_res = sb("x_res", [P, 2, D])
        x2 = sb("x2", [P, 2, D])

        ln2_part = sb("ln2_part", [P, 2, 6])
        ln2_mv = sb("ln2_mv", [P, 2, 2])
        cen = sb("cen", [P, 2, D])
        cen_max = sb("cen_max", [P, 2])
        row1 = sb("row1", [P, ROW1, 2])
        g_sq = sb("g_sq", [P, F], BF16)
        g_ssq = sb("g_ssq", [P, 2])
        g_max = sb("g_max", [P, 2])
        row2 = sb("row2", [P, ROW2, 2])

        wqk_in, wvo_in, wff_in, bqk_in, bias_in = (sem(n) for n in ("wqk_in", "wvo_in", "wff_in", "bqk_in", "bias_in"))
        ctx_in = [sem("ctx_in_0"), sem("ctx_in_1")]
        x_in_done, stored = sem("x_in_done"), sem("stored")
        x_res_in = [sem("x_res_in_0"), sem("x_res_in_1")]
        bv_spread, doubt_cleared = sem("bv_spread"), sem("doubt_cleared")
        const_ready, ident_ready = sem("const_ready"), sem("ident_ready")
        prep_ready, prep_taken = sem("prep_ready"), sem("prep_taken")
        wsum_ready, ternary_ready, wscale_step = sem("wsum_ready"), sem("ternary_ready"), sem("wscale_step")
        ln1_step, ln1_row, xn_ready, q_high_ready = sem("ln1_step"), sem("ln1_row"), sem("xn_ready"), sem("q_high_ready")
        wk_low_ready, ctx_low_ready, wvo_low_ready = sem("wk_low_ready"), sem("ctx_low_ready"), sem("wvo_low_ready")
        k_low_ready, q_low_ready, first_q_ready = sem("k_low_ready"), sem("q_low_ready"), sem("first_q_ready")
        s_ready, s_copied, cand_ready, max_ready = sem("s_ready"), sem("s_copied"), sem("cand_ready"), sem("max_ready")
        topk_step, settle_step, general_step = sem("topk_step"), sem("settle_step"), sem("general_step")
        e_ready, masked, p_ready = sem("e_ready"), sem("masked"), sem("p_ready")
        turned, turn_taken, xn_turned = sem("turned"), sem("turn_taken"), sem("xn_turned")
        result_ready, result_taken = sem("result_ready"), sem("result_taken")
        x2_step, xb_ready, bo_ready = sem("x2_step"), sem("xb_ready"), sem("bo_ready")
        row1_step, y1_ready, x2b_ready = sem("row1_step"), sem("y1_ready"), sem("x2b_ready")
        x2_kept_ready = sem("x2_kept_ready")
        g_ready, g_sq_ready, g_max_ready = sem("g_ready"), sem("g_sq_ready"), sem("g_max_ready")
        row2_step, y2_ready = sem("row2_step"), sem("y2_ready")

        JOB_WQK = 0
        JOB_CTX = JOB_WQK + 2
        NCTX = -(-SB // 2)
        JOB_Q0 = JOB_CTX + NCTX
        JOB_K = JOB_Q0 + 2
        JOB_MEAN = JOB_K + SC * DC
        JOB_WO = JOB_MEAN + 1
        JOB_Q1 = JOB_WO + 1
        JOB_WVO = JOB_Q1 + 2
        JOB_BVO = JOB_WVO + 1
        JOB_VO = JOB_BVO + 1
        JOB_W1 = JOB_VO + NCTX
        JOB_W2 = JOB_W1 + 4
        PREPS = JOB_W2 + 4

        def taken_before(n):
            return n - (n > JOB_Q0 + 1) - (n > JOB_MEAN) - (n > JOB_Q1 + 1)


        def taken_queries(j):
            if isinstance(j, int) and j == 2:
                return NT + 3 + DC
            return NT + (2 * NT + 2 + DC) + (j - 3) * TURNS + 3 + DC


        def taken_h(j, u):
            last = isinstance(j, int) and j == PAIRS - 1
            return j * RESULTS + (2 if last else 5) + 2 * u

        def taken_out(j, u):
            left = PAIRS - 1 - j if isinstance(j, int) else PAIRS
            return j * RESULTS + (7 if left == 0 else 13 if left == 1 else 10) + u

        waits_passed = {"pool": sem("pool_waits_passed"), "dve": sem("dve_waits_passed")}

        def wait_apart(engine, semaphore, value):
            engine.wait_ge(semaphore, value)
            if not isinstance(value, int):
                engine.sem_inc(waits_passed["pool" if engine.engine == nc.gpsimd.engine else "dve"], 1)

        block = stack.enter_context(nc.Block())

        @block.sync
        def _(sp):
            def w_load(n, W, s):
                sp.dma_start(W_rows[n][:, :, :], W.rearrange("(c p) d -> p c d", p=P)).then_inc(s, 16)

            w_load("k", Wk, wqk_in)
            w_load("q", Wq, wqk_in)
            full = SB - 1
            half = full // 2
            sp.dma_start(ctx_sb[:, 0:half, :],
                         ctx_rows[0:half * P, :].rearrange("(b p) d -> p b d", p=P)).then_inc(ctx_in[0], 16)
            for u in range(2):
                sp.dma_start(x_in[:, u, :], x_rows[u * P:(u + 1) * P, :]).then_inc(x_in_done, 16)
            sp.dma_start(ctx_sb[:, half:full, :],
                         ctx_rows[half * P:full * P, :].rearrange("(b p) d -> p b d", p=P)).then_inc(ctx_in[1], 16)
            sp.dma_start(ctx_sb[0:S_LAST, full, :], ctx_rows[full * P:S, :]).then_inc(ctx_in[1], 16)
            w_load("v", Wv, wvo_in)
            w_load("o", Wo, wvo_in)
            sp.dma_start(w1_sb[:, :, :], w1.rearrange("(b p) d -> p b d", p=P)).then_inc(wff_in, 16)
            sp.dma_start(w2_sb[:, :, :], w2.rearrange("(c p) f -> p c f", p=P)).then_inc(wff_in, 16)
            for u in range(2):
                sp.dma_start(x_res[:, u, :], x_rows[u * P:(u + 1) * P, :]).then_inc(x_res_in[u], 16)

            def load_x(j):
                for u in range(2):
                    sp.wait_ge(xn_ready, j * 2 + u - 1)
                    sp.dma_start(x_in[:, u, :], x_rows[bass.ds((j * 2 + u) * P, P), :]).then_inc(x_in_done, 16)

            def load_residual(t, u):
                sp.wait_ge(x2_step, (t - 2) * X2S + 2)
                sp.dma_start(x_res[:, u, :], x_rows[bass.ds(t * P, P), :]).then_inc(x_res_in[u], 16)

            load_x(1)

            def do_round(r, stage):
                if stage + 2 < PAIRS:
                    load_x(r + 2)
                if 1 <= stage < PAIRS:
                    load_residual(r * 2 + 1, 1)
                if stage >= 2:
                    for u in range(2):
                        sp.wait_ge(result_taken, taken_out(r - 2, u))
                        sp.dma_start(out_rows[bass.ds(((r - 2) * 2 + u) * P, P), :], o_sb[:, u, :]).then_inc(stored, 16)
                if stage + 1 < PAIRS:
                    load_residual(r * 2 + 2, 0)

            rounds(sp, do_round)
            sp.wait_ge(stored, 16 * TILES)

        @block.gpsimd
        def _(pool):
            pool.memset(ident[:, :], 0.0).then_inc(ident_ready, 1)
            pool.wait_ge(ident_ready, 1)
            pool.affine_select(out=ident[:, :], in_=ident[:, :], compare_op=ALU.not_equal, fill=1.0,
                               base=0, pattern=[[-1, P]], channel_multiplier=1).then_inc(ident_ready, 1)
            pool.memset(minus_half[:, :], -0.5).then_inc(const_ready, 1)
            pool.memset(minus_one[:, :], -1.0).then_inc(const_ready, 1)
            pool.memset(magic_col[:, :], MAGIC).then_inc(const_ready, 1)
            pool.memset(unmagic_col[:, :], -MAGIC).then_inc(const_ready, 1)
            pool.memset(ones[:, :], 1.0).then_inc(const_ready, 1)
            pool.memset(vo[:, :, D:DV], 1.0).then_inc(const_ready, 1)
            pool.dma_start(bv_col[:, :], bv.rearrange("(c p) -> p c", p=P),
                           allow_slow_non_contiguous=True).then_inc(bias_in, 16)
            pool.dma_start(bo_bc[:, :], bo.partition_broadcast(P)).then_inc(bias_in, 16)
            pool.dma_start(b1_bc[:, :], b1.partition_broadcast(P)).then_inc(bias_in, 16)
            pool.dma_start(b2_bc[:, :], b2.partition_broadcast(P)).then_inc(bias_in, 16)
            pool.wait_ge(const_ready, 6)

            def normalise(j):
                wait_apart(pool, ln1_step, (j + 1) * 4)
                pool.tensor_scalar(ln1_r[:, 0, :], ln1_mv[:, :, 1], EPS, None, ALU.add).then_inc(ln1_row, 1)
                pool.wait_ge(ln1_row, j * 2 + 1)
                pool.tensor_tensor(ln1_r[:, 1, :], ln1_r[:, 0, :], minus_half[:, :], ALU.pow).then_inc(ln1_row, 1)
                wait_apart(pool, ln1_row, j * 2 + 2)
                for u in range(2):
                    pool.tensor_scalar(xn[:, u, :], x_in[:, u, :], ln1_mv[:, u, 0:1], ln1_r[:, 1, u:u + 1],
                                       ALU.subtract, ALU.mult).then_inc(xn_ready, 1)

            def residual(t, u):
                pool.wait_ge(x_res_in[u], (t // 2 + 1) * 16 if isinstance(t, int) else t * 8 + (16 - 8 * u))
                pool.tensor_tensor(x_res[:, u, :], x_res[:, u, :], bo_bc[:, :], ALU.add).then_inc(xb_ready, 1)

            def row_scales_1(j):
                mean_var, base = ln2_mv, j * ROW1
                wait_apart(pool, x2_step, (j + 1) * 2 * X2S)
                n = [0]

                def step(ins):
                    ins.then_inc(row1_step, 1)
                    n[0] += 1
                    wait_apart(pool, row1_step, base + n[0])

                shifted, r, z, step_size, inverse, sc, dq = (row1[:, k, :] for k in range(7))
                step(pool.tensor_scalar(shifted, mean_var[:, :, 1], 1.0 + EPS, EPS * EPS, ALU.mult, ALU.add))
                step(pool.tensor_tensor(r, shifted, minus_half[:, :], ALU.pow))
                step(pool.tensor_tensor(z, r, cen_max[:, :], ALU.mult))
                step(pool.tensor_scalar(step_size, z, 1e-5, 1.0 / 127.0, ALU.max, ALU.mult))
                step(pool.tensor_tensor(inverse, step_size, minus_one[:, :], ALU.pow))
                step(pool.tensor_tensor(sc, inverse, r, ALU.mult))
                step(pool.tensor_scalar(dq, step_size, wmean[:, 0:1], None, ALU.mult))

            def quantise_1(j):
                for u in range(2):
                    pool.tensor_scalar(y1[:, u, :], cen[:, u, :], row1[:, 5, u:u + 1], MAGIC,
                                       ALU.mult, ALU.add).then_inc(y1_ready, 1)

            def keep_residual(j):
                if not isinstance(j, int) or j > 0:
                    pool.wait_ge(x2b_ready, j * 2)
                for u in range(2):
                    pool.tensor_tensor(x2_kept[:, u, :], x2[:, u, :], b2_bc[:, :], ALU.add).then_inc(x2_kept_ready, 1)

            def move_residual(j):
                if not isinstance(j, int) or j > 0:
                    pool.wait_ge(result_taken, taken_out(j - 1, 1))
                wait_apart(pool, x2_kept_ready, (j + 1) * 2)
                pool.tensor_copy(x2b[:, :, :], x2_kept[:, :, :]).then_inc(x2b_ready, 2)

            def row_scales_2(j):
                base = j * ROW2
                pool.wait_ge(g_sq_ready, (j + 1) * 2)
                wait_apart(pool, g_max_ready, (j + 1) * 2)
                n = [0]

                def step(ins):
                    ins.then_inc(row2_step, 1)
                    n[0] += 1
                    wait_apart(pool, row2_step, base + n[0])

                mean_sq, r, z, step_size, inverse, sc, dq = (row2[:, k, :] for k in range(7))
                step(pool.tensor_scalar(mean_sq, g_ssq[:, :], 1.0 / F, EPS, ALU.mult, ALU.add))
                step(pool.tensor_tensor(r, mean_sq, minus_half[:, :], ALU.pow))
                step(pool.tensor_tensor(z, r, g_max[:, :], ALU.mult))
                step(pool.tensor_scalar(step_size, z, 1e-5, 1.0 / 127.0, ALU.max, ALU.mult))
                step(pool.tensor_tensor(inverse, step_size, minus_one[:, :], ALU.pow))
                step(pool.tensor_tensor(sc, inverse, r, ALU.mult))
                step(pool.tensor_scalar(dq, step_size, wmean[:, 1:2], None, ALU.mult))

            def split_queries(j):
                pool.wait_ge(q_high_ready, (j + 1) * DC)
                if isinstance(j, int) and j <= 1:
                    pool.wait_ge(first_q_ready, (j + 1) * DC)
                else:
                    pool.wait_ge(turn_taken, taken_queries(j))
                pool.tensor_tensor(q_low[:, :, :], q_full[:, :, :], q_high[:, :, :],
                                   ALU.subtract).then_inc(q_low_ready, 1)

            normalise(0)
            split_queries(0)
            normalise(1)
            split_queries(1)
            pool.wait_ge(wscale_step, 2)
            pool.wait_ge(bias_in, 4 * 16)
            pool.wait_ge(prep_taken, taken_before(JOB_BVO + 1))
            pool.tensor_tensor(bo_bc[:, :], bo_bc[:, :], bvo_bc[:, :], ALU.add).then_inc(bo_ready, 1)
            pool.wait_ge(bo_ready, 1)
            residual(0, 0)

            def do_round(r, stage):
                if 1 <= stage and stage + 1 < PAIRS:
                    split_queries(r + 1)
                if stage >= 2:
                    move_residual(r - 2)
                if stage + 2 < PAIRS:
                    pool.wait_ge(xn_turned, r + 1)
                    normalise(r + 2)
                if stage == PAIRS:
                    row_scales_1(r - 1)
                    quantise_1(r - 1)
                if stage >= 2:
                    row_scales_2(r - 2)
                if 1 <= stage < PAIRS:
                    row_scales_1(r - 1)
                    quantise_1(r - 1)
                if 1 <= stage <= PAIRS:
                    keep_residual(r - 1)
                if stage < PAIRS:
                    residual(r * 2 + 1, 1)
                if stage + 1 < PAIRS:
                    residual(r * 2 + 2, 0)

            rounds(pool, do_round)

        @block.scalar
        def _(act):
            def taken(n, dst, src, **how):
                act.wait_ge(prep_ready, n + 1)
                act.activation(dst, src, ACT.Identity, **how).then_inc(prep_taken, 1)

            def bank(n):
                return prep[n % 4]

            def copy_scores(t, u, c):
                at, n = CHUNKS[c]
                act.wait_ge(s_ready, t * SC + c + 1)
                act.activation(s_sb[:, u, at:at + n], score[c][:, 0:n], ACT.Copy).then_inc(s_copied, 1)

            def take_queries(o, src, taken):
                act.activation(q_high[:, o, :], src, ACT.Identity, bias=bq_col[:, o:o + 1]).then_inc(q_high_ready, 1)
                act.activation(q_full[:, o, :], src, ACT.Identity, bias=bq_col[:, o:o + 1]).then_inc(taken, 1)

            for column, b in ((bk_col, bk), (bq_col, bq)):
                act.dma_start(column[:, :], b.rearrange("(c p) -> p c", p=P),
                              allow_slow_non_contiguous=True).then_inc(bqk_in, 16)
            act.wait_ge(const_ready, 6)
            for k, w in enumerate((wk_high, WT["q"])):
                taken(JOB_WQK + k, w[:, :, :], bank(JOB_WQK + k)[:, :].rearrange("p (c o) -> p c o", c=DC))
            for k in range(NCTX):
                n = min(2 * P, S - 2 * k * P)
                src = bank(JOB_CTX + k)[:, :].rearrange("p (c s) -> p c s", c=DC)[:, :, 0:n]
                taken(JOB_CTX + k, ctx_high[:, :, 2 * k * P:2 * k * P + n], src)
            act.wait_ge(bqk_in, 2 * 16)

            def take_first(n, j):
                taken(n, xnT[:, :, :], bank(n)[:, :].rearrange("p (c t) -> p c t", c=DC))
                act.wait_ge(prep_ready, n + 2)
                if j:
                    act.wait_ge(q_low_ready, j)
                for o in range(DC):
                    take_queries(o, bank(n + 1)[:, o * 2 * P:(o + 1) * 2 * P], first_q_ready)

            def exp_all(t, u):
                act.wait_ge(max_ready, t + 1)
                act.activation(e_all[:, u, :], s_sb[:, u, :], ACT.Exp, bias=neg_max[:, u:u + 1],
                               scale=SCALE).then_inc(e_ready, 1)

            take_first(JOB_Q0, 0)
            for k in range(SC * DC):
                (at, n), o = CHUNKS[k // DC], k % DC
                taken(JOB_K + k, k_high[:, o, at:at + n], bank(JOB_K + k)[:, 0:n], bias=bk_col[:, o:o + 1])
            for c in range(SC):
                copy_scores(0, 0, c)
            for c in range(SC):
                copy_scores(1, 1, c)
            taken(JOB_WO, WT["o"][:, :, :], bank(JOB_WO)[:, :].rearrange("p (c o) -> p c o", c=DC))
            take_first(JOB_Q1, 1)
            taken(JOB_WVO, wvo_high[:, :, :], bank(JOB_WVO)[:, :].rearrange("p (c o) -> p c o", c=DC))
            taken(JOB_BVO, bvo_bc[:, :], bank(JOB_BVO)[:, 0:D])
            for k in range(NCTX):
                if k == 1:
                    exp_all(0, 0)
                nb = min(2, SB - 2 * k)
                rows = P if 2 * k + nb < SB else S_LAST
                taken(JOB_VO + k, vo[0:rows, 2 * k:2 * k + nb, 0:D],
                      bank(JOB_VO + k)[0:rows, 0:nb * D].rearrange("p (b d) -> p b d", b=nb))
            for k in range(4):
                b = k % 2 * 4
                taken(JOB_W1 + k, w1T[:, k // 2, b * P:(b + 4) * P], bank(JOB_W1 + k)[:, :], bias=unmagic_col[:, 0:1])
            for k in range(4):
                c, b = k // 2, k % 2 * 4
                taken(JOB_W2 + k, w2T[:, b:b + 4, c * P:(c + 1) * P],
                      bank(JOB_W2 + k)[:, :].rearrange("p (b o) -> p b o", b=4), bias=unmagic_col[:, 0:1])
            exp_all(1, 1)

            turns = Count(TURNS)

            def take_turn(dst, cols, parts=1, bias=None):
                k = turns.before % 2
                act.wait_ge(turned, turns.next() + 1)
                src = turn[k][0:dst.shape[0], 0:cols]
                if parts > 1:
                    src = src.rearrange("p (b n) -> p b n", b=parts)
                if bias is None:
                    act.activation(dst, src, ACT.Copy).then_inc(turn_taken, 1)
                else:
                    act.activation(dst, src, ACT.Identity, bias=bias).then_inc(turn_taken, 1)

            def take_weights(q):
                lo, hi = QUADS[q]
                rows = P if hi < SB else S_LAST
                take_turn(pT[0:rows, lo * P:hi * P], (hi - lo) * P)

            def do_round(r, stage):
                if 1 <= stage < PAIRS:
                    act.wait_ge(p_ready, r * 2)
                    for c in range(SC):
                        copy_scores(r * 2 + 1, 1, c)
                if 1 <= stage and stage + 1 < PAIRS:
                    take_turn(xnT[:, :, :], 2 * D, DC)
                if 1 <= stage <= PAIRS:
                    take_weights(0)
                    take_weights(1)
                if 1 <= stage < PAIRS:
                    exp_all(r * 2, 0)
                if 1 <= stage and stage + 1 < PAIRS:
                    act.wait_ge(q_low_ready, r + 1)
                    for o in range(DC):
                        k = turns.before % 2
                        act.wait_ge(turned, turns.next() + 1)
                        take_queries(o, turn[k][:, 0:2 * P], turn_taken)
                if 1 <= stage <= PAIRS:
                    take_weights(2)
                    take_weights(3)
                if stage >= 2:
                    for u in range(2):
                        act.wait_ge(result_taken, taken_h(r - 2, u))
                        act.activation(g_of(stage - 2)[:, u, :], g_of(stage - 2)[:, u, :], ACT.Gelu).then_inc(g_ready, 1)
                    for u in range(2):
                        act.wait_ge(g_ready, (r - 2) * 2 + u + 1)
                        if u or stage >= 3:
                            act.wait_ge(g_sq_ready, (r - 2) * 2 + u)
                        act.activation(g_sq[:, :], g_of(stage - 2)[:, u, :], ACT.Square,
                                       accum_out=g_ssq[:, u:u + 1]).then_inc(g_sq_ready, 1)
                if stage + 1 < PAIRS:
                    act.wait_ge(p_ready, r * 2 + 1)
                    for c in range(SC):
                        copy_scores(r * 2 + 2, 0, c)
                if stage < PAIRS:
                    take_weights(0)
                    take_weights(1)
                if 1 <= stage < PAIRS:
                    exp_all(r * 2 + 1, 1)
                if stage < PAIRS:
                    take_weights(2)
                    take_weights(3)
                if stage == PAIRS:
                    take_turn(y1T[:, :, :], 2 * D, DC, unmagic_col[:, 0:1])
                if stage >= 2:
                    act.wait_ge(row2_step, (r - 1) * ROW2)
                    for u in range(2):
                        act.activation(y2[:, u, :], g_of(stage - 2)[:, u, :], ACT.Identity, scale=row2[:, 5, u:u + 1],
                                       bias=magic_col[:, 0:1]).then_inc(y2_ready, 1)
                    for u in range(2):
                        for h in range(2):
                            take_turn(y2T[:, h * 4:h * 4 + 4, u * P:(u + 1) * P], BANK, 4, unmagic_col[:, 0:1])
                if 1 <= stage < PAIRS:
                    take_turn(y1T[:, :, :], 2 * D, DC, unmagic_col[:, 0:1])

            rounds(act, do_round, [turns])

        @block.vector
        def _(dve):
            def ln1_part_stats(j):
                dve.wait_ge(x_in_done, (j + 1) * 32)
                for u in range(2):
                    dve.bn_stats(ln1_part[:, u, :], x_in[:, u, :]).then_inc(ln1_step, 1)

            def ln1_stats(j):
                for u in range(2):
                    wait_apart(dve, ln1_step, j * 4 + u + 1)
                    dve.bn_aggr(ln1_mv[:, u, :], ln1_part[:, u, :]).then_inc(ln1_step, 1)

            def candidates(t, u, part=0, parts=1):
                if part == 0:
                    wait_apart(dve, s_copied, (t + 1) * SC)
                for k in range(part * PIECES // parts, (part + 1) * PIECES // parts):
                    end = (k + 1) * PIECE if k < PIECES - 1 else S
                    ins = dve.max(cand[:, u, 8 * k:8 * k + 8], s_sb[:, u, k * PIECE:end])
                if part == parts - 1:
                    ins.then_inc(cand_ready, 1)

            TOPK_STEPS = 2 * ROUNDS - 1

            def best_8(t, u, k):
                if k == 0:
                    wait_apart(dve, cand_ready, t + 1)
                else:
                    wait_apart(dve, topk_step, t * TOPK_STEPS + 2 * k)
                dve.max(best[:, k, :], cand_left[:, :] if k else cand[:, u, :]).then_inc(topk_step, 1)
                if k == 0:
                    dve.wait_ge(topk_step, t * TOPK_STEPS + 1)
                    dve.tensor_scalar(neg_max[:, u:u + 1], best[:, 0, 0:1], -SCALE, None,
                                      ALU.mult).then_inc(max_ready, 1)

            def drop_8(t, u, k):
                wait_apart(dve, topk_step, t * TOPK_STEPS + 2 * k + 1)
                dve.match_replace(cand_left[:, :], best[:, k, :], cand_left[:, :] if k else cand[:, u, :],
                                  LOWEST).then_inc(topk_step, 1)

            SETTLE_STEPS = 8

            def settled(t, n):
                dve.wait_ge(settle_step, t * SETTLE_STEPS + n)

            def weigh(t, u):
                dve.wait_ge(topk_step, (t + 1) * TOPK_STEPS)
                dve.wait_ge(e_ready, t + 1)
                dve.scalar_tensor_tensor(e_all[:, u, :], s_sb[:, u, :], best[:, ROUNDS - 1, 7:8], e_all[:, u, :],
                                         ALU.is_ge, ALU.mult).then_inc(masked, 1)

            def settle(t, u, n):
                least = best[:, ROUNDS - 1, 7:8]
                if n == 0:
                    dve.tensor_scalar(cand_ge[:, :], cand[:, u, :], least, 0.0, ALU.is_ge, ALU.add,
                                      accum_out=counts[:, 0:1]).then_inc(settle_step, 1)
                if n == 1:
                    settled(t, 1)
                    dve.tensor_scalar(cand_ge[:, 0:PIECES], cand[:, u, 7:CAND:8], least, 0.0, ALU.is_ge, ALU.add,
                                      accum_out=counts[:, 1:2]).then_inc(settle_step, 1)
                if n == 2:
                    settled(t, 2)
                    dve.scalar_tensor_tensor(doubt[:, 0:1], counts[:, 0:1], float(TOPK), counts[:, 1:2], ALU.subtract,
                                             ALU.add).then_inc(settle_step, 1)
                if n == 3:
                    settled(t, 3)
                    dve.transpose(doubt_row[:, 0:32], doubt[:, :]).then_inc(settle_step, 1)
                if n == 4:
                    settled(t, 4)
                    for k in range(1, 4):
                        dve.tensor_copy(doubt_row[0:1, 32 * k:32 * k + 32],
                                        doubt_row[32 * k:32 * k + 1, 0:32]).then_inc(settle_step, 1)
                if n == 5:
                    settled(t, 7)
                    dve.tensor_reduce(doubtful[:, u:u + 1], doubt_row[0:1, :], AX.X, ALU.max).then_inc(settle_step, 1)

            def release(t, u):
                wait_apart(dve, settle_step, (t + 1) * SETTLE_STEPS)
                left = dve.value_load(doubtful[0:1, u:u + 1], min_val=0, max_val=2 * CAND)
                with dve.If(left > 0):
                    dve.sem_clear(general_step)
                    for k in range(ROUNDS):
                        src = s_left[:, :] if k else s_sb[:, u, :]
                        if k:
                            dve.wait_ge(general_step, 2 * k)
                        dve.max(best_of_all[:, :], src).then_inc(general_step, 1)
                        dve.wait_ge(general_step, 2 * k + 1)
                        dve.match_replace(s_left[:, :], best_of_all[:, :], src, LOWEST).then_inc(general_step, 1)
                    dve.wait_ge(general_step, 2 * ROUNDS)
                    dve.wait_ge(masked, t + 1)
                    dve.scalar_tensor_tensor(e_all[:, u, :], s_left[:, :], LOWEST, e_all[:, u, :], ALU.is_equal,
                                             ALU.mult).then_inc(general_step, 1)
                    dve.wait_ge(general_step, 2 * ROUNDS + 1)
                with dve.Else():
                    pass
                dve.wait_ge(masked, t + 1)
                dve.sem_inc(p_ready, 1)

            results = Count(RESULTS)

            def take_result():
                k, n = results.before % 2, results.next() + 1
                dve.wait_ge(result_ready, n)
                return result[k], n

            def attended(t, u, n):
                base = t * X2S
                if n == 0:
                    x2_bank[0], x2_bank[1] = take_result()
                    dve.wait_ge(xb_ready, t + 1)
                    dve.reciprocal(inv_sum[:, u:u + 1], x2_bank[0][:, D:DV]).then_inc(x2_step, 1)
                if n == 1:
                    if not isinstance(t, int) or t >= 2:
                        dve.wait_ge(x2_kept_ready, t - u)
                    dve.wait_ge(x2_step, base + 1)
                    dve.scalar_tensor_tensor(x2[:, u, :], x2_bank[0][:, 0:D], inv_sum[:, u:u + 1], x_res[:, u, :],
                                             ALU.mult, ALU.add).then_inc(result_taken, 1)
                if n == 2:
                    dve.wait_ge(result_taken, x2_bank[1])
                    dve.bn_stats(ln2_part[:, u, :], x2[:, u, :]).then_inc(x2_step, 1)
                if n == 3:
                    wait_apart(dve, x2_step, base + 2)
                    dve.bn_aggr(ln2_mv[:, u, :], ln2_part[:, u, :]).then_inc(x2_step, 1)
                if n == 4:
                    dve.wait_ge(x2_step, base + 3)
                    dve.tensor_scalar(cen[:, u, :], x2[:, u, :], ln2_mv[:, u, 0:1], None,
                                      ALU.subtract).then_inc(x2_step, 1)
                if n == 5:
                    dve.wait_ge(x2_step, base + 4)
                    dve.tensor_reduce(cen_max[:, u:u + 1], cen[:, u, :], AX.X, ALU.max,
                                      apply_absolute_value=True).then_inc(x2_step, 1)

            x2_bank = [None, None]
            X2_PARTS, SETTLE_PARTS = 6, 6
            PARTS = SETTLE_PARTS + X2_PARTS

            def hidden(j):
                dve.wait_ge(row1_step, (j + 1) * ROW1)
                for u in range(2):
                    for h in range(2):
                        bank, _ = take_result()
                        dve.scalar_tensor_tensor(g_of(j)[:, u, h * BANK:(h + 1) * BANK], bank[:, :], row1[:, 6, u:u + 1],
                                                 b1_bc[:, h * BANK:(h + 1) * BANK], ALU.mult,
                                                 ALU.add).then_inc(result_taken, 1)

            def gelu_max(j, u):
                dve.wait_ge(g_ready, j * 2 + u + 1)
                dve.tensor_reduce(g_max[:, u:u + 1], g_of(j)[:, u, :], AX.X, ALU.max,
                                  apply_absolute_value=True).then_inc(g_max_ready, 1)

            def output(j, u):
                dve.wait_ge(x2b_ready, (j + 1) * 2)
                if not isinstance(j, int) or j > 0:
                    dve.wait_ge(stored, j * 32)
                bank, _ = take_result()
                dve.scalar_tensor_tensor(o_sb[:, u, :], bank[:, 0:D], row2[:, 6, u:u + 1],
                                         x2b[:, u, :], ALU.mult, ALU.add).then_inc(result_taken, 1)

            dve.memset(doubt[:, :], 0.0).then_inc(doubt_cleared, 1)
            dve.wait_ge(doubt_cleared, 1)
            ln1_part_stats(0)
            ln1_stats(0)
            dve.wait_ge(const_ready, 6)
            for part in (ctx_high, ctx_low):
                dve.memset(part[:, :, S:S_EVEN].bitcast(F32), 0.0).then_inc(ctx_low_ready, 1)

            def leave_low(n, low, high, bank, ready):
                dve.wait_ge(prep_taken, taken_before(n + 1))
                dve.tensor_tensor(low, bank, high, ALU.subtract).then_inc(ready, 1)

            def two_chunks(n, width=D):
                return prep[n % 4][:, :].rearrange("p (c o) -> p c o", c=DC)[:, :, 0:width]

            leave_low(JOB_WQK, wk_low[:, :, :], wk_high[:, :, :], two_chunks(JOB_WQK), wk_low_ready)
            for k in range(NCTX):
                at, n = 2 * k * P, min(2 * P, S - 2 * k * P)
                leave_low(JOB_CTX + k, ctx_low[:, :, at:at + n], ctx_high[:, :, at:at + n],
                          two_chunks(JOB_CTX + k, n), ctx_low_ready)
            for part in (k_high, k_low):
                dve.memset(part[:, :, S:S_EVEN].bitcast(F32), 0.0).then_inc(k_low_ready, 1)
            dve.wait_ge(bqk_in, 2 * 16)
            for k in range(SC * DC):
                (at, n), o = CHUNKS[k // DC], k % DC
                dve.wait_ge(prep_taken, taken_before(JOB_K + k + 1))
                dve.scalar_tensor_tensor(k_low[:, o, at:at + n], prep[(JOB_K + k) % 4][:, 0:n], bk_col[:, o:o + 1],
                                         k_high[:, o, at:at + n], ALU.add, ALU.subtract).then_inc(k_low_ready, 1)
            dve.wait_ge(bias_in, 4 * 16)
            for c in range(DC):
                dve.tensor_scalar(bv_bc[:, c, :], ones[:, :], bv_col[:, c:c + 1], None, ALU.mult).then_inc(bv_spread, 1)
            ln1_part_stats(1)
            ln1_stats(1)
            dve.wait_ge(wff_in, 32)
            for k, w in enumerate((w1_sb, w2_sb)):
                dve.tensor_reduce(wsum[:, k:k + 1], w[:, :, :], AX.XY, ALU.add,
                                  apply_absolute_value=True).then_inc(wsum_ready, 1)
            candidates(0, 0)
            best_8(0, 0, 0)
            dve.wait_ge(prep_ready, JOB_MEAN + 1)
            dve.tensor_scalar(wmean[:, :], prep[JOB_MEAN % 4][:, 0:2], 1.0 / (D * F), 1e-5,
                              ALU.mult, ALU.max).then_inc(wscale_step, 1)
            dve.wait_ge(wscale_step, 1)
            dve.reciprocal(winv[:, :], wmean[:, :]).then_inc(wscale_step, 1)
            dve.wait_ge(wscale_step, 2)
            for k, w in enumerate((w1_sb, w2_sb)):
                dve.tensor_scalar(w[:, :, :], w[:, :, :], winv[:, k:k + 1], MAGIC, ALU.mult,
                                  ALU.add).then_inc(wscale_step, 1)
                dve.wait_ge(wscale_step, 3 + k)
                dve.tensor_scalar(w[:, :, :], w[:, :, :], MAGIC + 1.0, MAGIC - 1.0, ALU.min,
                                  ALU.max).then_inc(ternary_ready, 1)
                if k == 0:
                    leave_low(JOB_WVO, wvo_low[:, :, :], wvo_high[:, :, :], two_chunks(JOB_WVO), wvo_low_ready)

            def do_round(r, stage):
                attention, x2_now, late = stage < PAIRS, 1 <= stage <= PAIRS, 2 <= stage
                if 1 <= stage < PAIRS:
                    best_8(r * 2, 0, 0)
                if attention:
                    drop_8(r * 2, 0, 0)
                    best_8(r * 2, 0, 1)
                    drop_8(r * 2, 0, 1)
                    best_8(r * 2, 0, 2)
                if stage + 2 < PAIRS:
                    ln1_part_stats(r + 2)
                if attention:
                    drop_8(r * 2, 0, 2)
                if stage + 2 < PAIRS:
                    ln1_stats(r + 2)
                if attention:
                    best_8(r * 2, 0, 3)
                    weigh(r * 2, 0)
                    for n in range(PARTS):
                        candidates(r * 2 + 1, 1, n, PARTS)
                        if n < SETTLE_PARTS:
                            settle(r * 2, 0, n)
                    release(r * 2, 0)
                if stage == PAIRS:
                    for n in range(X2_PARTS):
                        attended(r * 2 - 1, 1, n)
                    x2_now = False
                if late:
                    gelu_max(r - 2, 0)
                    gelu_max(r - 2, 1)
                if x2_now:
                    attended(r * 2 - 1, 1, 0)
                if attention:
                    best_8(r * 2 + 1, 1, 0)
                if x2_now:
                    attended(r * 2 - 1, 1, 1)
                if attention:
                    drop_8(r * 2 + 1, 1, 0)
                if x2_now:
                    attended(r * 2 - 1, 1, 2)
                if attention:
                    best_8(r * 2 + 1, 1, 1)
                if x2_now:
                    attended(r * 2 - 1, 1, 3)
                if attention:
                    drop_8(r * 2 + 1, 1, 1)
                if x2_now:
                    attended(r * 2 - 1, 1, 4)
                if attention:
                    best_8(r * 2 + 1, 1, 2)
                if x2_now:
                    attended(r * 2 - 1, 1, 5)
                if attention:
                    drop_8(r * 2 + 1, 1, 2)
                if attention:
                    best_8(r * 2 + 1, 1, 3)
                    weigh(r * 2 + 1, 1)
                for n in range(PARTS):
                    if stage + 1 < PAIRS:
                        candidates(r * 2 + 2, 0, n, PARTS)
                    if attention and n < SETTLE_PARTS:
                        settle(r * 2 + 1, 1, n)
                    if attention and n >= PARTS - X2_PARTS:
                        attended(r * 2, 0, n - (PARTS - X2_PARTS))
                if attention:
                    release(r * 2 + 1, 1)
                if stage == PAIRS:
                    hidden(r - 1)
                if late:
                    output(r - 2, 0)
                    output(r - 2, 1)
                if x2_now:
                    hidden(r - 1)

            rounds(dve, do_round, [results])

        @block.tensor
        def _(pe):
            def prep_bank(n):
                if n >= 4:
                    pe.wait_ge(prep_taken, taken_before(n - 3))
                if n - 4 == JOB_WQK:
                    pe.wait_ge(wk_low_ready, 1)
                if JOB_CTX <= n - 4 < JOB_Q0:
                    pe.wait_ge(ctx_low_ready, n - 4 - JOB_CTX + 1 + 2)
                if n - 4 == JOB_WVO:
                    pe.wait_ge(wvo_low_ready, 1)
                if JOB_K <= n - 4 < JOB_MEAN:
                    pe.wait_ge(k_low_ready, n - 4 - JOB_K + 1 + 2)
                if n - 4 in (JOB_Q0 + 1, JOB_Q1 + 1):
                    for q_ready in (q_high_ready, first_q_ready):
                        pe.wait_ge(q_ready, DC if n - 4 < JOB_Q1 else 2 * DC)
                if n - 4 == JOB_MEAN:
                    pe.wait_ge(wscale_step, 1)
                return prep[n % 4]

            def prep_turn(n, blocks):
                bank = prep_bank(n)
                for k, (src, at) in enumerate(blocks):
                    rows = src.shape[0]
                    ins = pe.transpose(bank[:, at:at + rows], src, ident[0:rows, 0:rows])
                ins.then_inc(prep_ready, 1)

            def weights_T(n, name):
                prep_turn(n, [(W_rows[name][:, o, c * P:(c + 1) * P], c * D + o * P)
                              for c in range(DC) for o in range(DC)])

            def product_of_parts(out, factors):
                steps = [(a, b) for ah, al, bh, bl in factors for a, b in ((al, bh), (ah, bl), (ah, bh))]
                for i, (a, b) in enumerate(steps):
                    ins = pe.matmul(out, a, b, start=(i == 0), stop=(i == len(steps) - 1))
                return ins

            def project_keys():
                for k in range(SC * DC):
                    (at, n), o = CHUNKS[k // DC], k % DC
                    n += n % 2
                    ws, cols = slice(o * P, (o + 1) * P), slice(at, at + n)
                    bank = prep_bank(JOB_K + k)
                    product_of_parts(
                        bank[:, 0:n], [(wk_high[:, c, ws], wk_low[:, c, ws], ctx_high[:, c, cols], ctx_low[:, c, cols])
                                       for c in range(DC)]).then_inc(prep_ready, 1)

            def scores(t, u, c):
                at, n = CHUNKS[c]
                n += n % 2
                if u or not isinstance(t, int) or t > 0:
                    pe.wait_ge(s_copied, (t - 1) * SC + c + 1)
                qs, cols = slice(u * P, (u + 1) * P), slice(at, at + n)
                product_of_parts(
                    score[c][:, 0:n], [(q_high[:, k, qs], q_low[:, k, qs], k_high[:, k, cols], k_low[:, k, cols])
                                       for k in range(DC)]).then_inc(s_ready, 1)

            pe.wait_ge(ident_ready, 2)
            pe.wait_ge(wqk_in, 32)
            weights_T(JOB_WQK, "k")
            weights_T(JOB_WQK + 1, "q")
            for k in range(NCTX):
                if k == 0:
                    pe.wait_ge(ctx_in[0], 16)
                if k == (SB - 1) // 2 // 2:
                    pe.wait_ge(ctx_in[1], 32)
                blocks = []
                for b in range(2 * k, min(2 * k + 2, SB)):
                    rows = P if b < SB - 1 else S_LAST
                    blocks += [(ctx_sb[0:rows, b, c * P:(c + 1) * P], c * D + (b - 2 * k) * P) for c in range(DC)]
                prep_turn(JOB_CTX + k, blocks)

            def first_queries(n, j):
                pe.wait_ge(xn_ready, (j + 1) * 2)
                prep_turn(n, [(xn[:, u, c * P:(c + 1) * P], c * D + u * P) for c in range(DC) for u in range(2)])
                bank = prep_bank(n + 1)
                pe.wait_ge(prep_taken, taken_before(n + 1))
                if j:
                    pe.sem_inc(xn_turned, 1)
                for o in range(DC):
                    for c in range(DC):
                        ins = pe.matmul(bank[:, o * 2 * P:(o + 1) * 2 * P], WT["q"][:, c, o * P:(o + 1) * P],
                                        xnT[:, c, :], start=(c == 0), stop=(c == DC - 1))
                ins.then_inc(prep_ready, 1)

            first_queries(JOB_Q0, 0)
            pe.wait_ge(ctx_low_ready, NCTX + 2)
            project_keys()
            pe.wait_ge(q_low_ready, 1)
            pe.wait_ge(k_low_ready, SC * DC + 2)
            for c in range(SC):
                scores(0, 0, c)
            pe.wait_ge(wsum_ready, 2)
            pe.wait_ge(const_ready, 6)
            pe.matmul(prep_bank(JOB_MEAN)[:, 0:2], ones[:, :], wsum[:, :], start=True, stop=True).then_inc(prep_ready, 1)
            for c in range(SC):
                scores(1, 1, c)
            pe.wait_ge(wvo_in, 32)
            weights_T(JOB_WO, "o")
            first_queries(JOB_Q1, 1)
            pe.wait_ge(prep_taken, taken_before(JOB_WO + 1))
            bank = prep_bank(JOB_WVO)
            for i in range(DC):
                for c in range(DC):
                    ins = pe.matmul(bank[:, i * D:(i + 1) * D], W_rows["v"][:, c, i * P:(i + 1) * P], WT["o"][:, c, :],
                                    start=(c == 0), stop=(c == DC - 1))
            ins.then_inc(prep_ready, 1)
            bank = prep_bank(JOB_BVO)
            pe.wait_ge(bv_spread, DC)
            for c in range(DC):
                ins = pe.matmul(bank[:, 0:D], bv_bc[:, c, :], WT["o"][:, c, :], start=(c == 0), stop=(c == DC - 1))
            ins.then_inc(prep_ready, 1)
            pe.wait_ge(q_high_ready, 2 * DC)
            pe.wait_ge(q_low_ready, 2)
            for c in range(SC):
                scores(2, 0, c)
            pe.wait_ge(prep_taken, taken_before(JOB_WVO + 1))
            pe.wait_ge(wvo_low_ready, 1)
            for k in range(NCTX):
                bank = prep_bank(JOB_VO + k)
                for b in range(2 * k, min(2 * k + 2, SB)):
                    rows = min(P, S_EVEN - b * P)
                    at, cols = (b - 2 * k) * D, slice(b * P, b * P + rows)
                    ins = product_of_parts(bank[0:rows, at:at + D],
                                [(ctx_high[:, c, cols], ctx_low[:, c, cols], wvo_high[:, c, :], wvo_low[:, c, :])
                                 for c in range(DC)])
                ins.then_inc(prep_ready, 1)
            pe.wait_ge(ternary_ready, 1)
            for k in range(4):
                c, b = k // 2, k % 2 * 4
                prep_turn(JOB_W1 + k, [(w1_sb[:, b + i, c * P:(c + 1) * P], i * P) for i in range(4)])
            pe.wait_ge(ternary_ready, 2)
            for k in range(4):
                c, b = k // 2, k % 2 * 4
                prep_turn(JOB_W2 + k, [(w2_sb[:, c, (b + i) * P:(b + i + 1) * P], i * P) for i in range(4)])
            pe.wait_ge(prep_taken, taken_before(PREPS))

            turns, results = Count(TURNS), Count(RESULTS)

            def turn_bank():
                k, first = turns.before % 2, turns.loop is None and turns.before < 2
                n = turns.next()
                if not first:
                    pe.wait_ge(turn_taken, n - 1)
                return turn[k]

            def result_bank():
                k, first = results.before % 2, results.loop is None and results.before < 2
                n = results.next()
                if not first:
                    pe.wait_ge(result_taken, n - 1)
                return result[k]

            def turn_weights(u, q):
                bank = turn_bank()
                lo, hi = QUADS[q]
                for b in range(lo, hi):
                    n = P if b < SB - 1 else S_LAST
                    ins = pe.transpose(bank[0:n, (b - lo) * P:(b - lo + 1) * P],
                                       e_all[:, u, b * P:b * P + n], ident[:, :])
                ins.then_inc(turned, 1)

            def weighted(bank, q, landed):
                pe.wait_ge(turn_taken, landed)
                lo, hi = QUADS[q]
                for b in range(lo, hi):
                    n = P if b < SB - 1 else S_LAST
                    ins = pe.matmul(bank[:, 0:DV], pT[0:n, b * P:(b + 1) * P], vo[0:n, b, :],
                                    start=(b == 0), stop=(b == SB - 1))
                return ins

            def turn_y2(u, h):
                bank = turn_bank()
                for k in range(4):
                    ins = pe.transpose(bank[:, k * P:(k + 1) * P], y2[:, u, (h * 4 + k) * P:(h * 4 + k + 1) * P],
                                       ident[:, :])
                ins.then_inc(turned, 1)

            def turn_pair(src):
                bank = turn_bank()
                for c in range(DC):
                    for u in range(2):
                        ins = pe.transpose(bank[:, c * D + u * P:c * D + (u + 1) * P], src[:, u, c * P:(c + 1) * P],
                                           ident[:, :])
                ins.then_inc(turned, 1)

            def turned_so_far():
                n = turns.before
                return n if turns.loop is None else (turns.loop - LOOP[0]) * TURNS + n

            def queries(o, xn_landed):
                bank = turn_bank()
                pe.wait_ge(turn_taken, xn_landed)
                for c in range(DC):
                    ins = pe.matmul(bank[:, 0:2 * P], WT["q"][:, c, o * P:(o + 1) * P], xnT[:, c, :],
                                    start=(c == 0), stop=(c == DC - 1))
                ins.then_inc(turned, 1)

            def up(u):
                for h in range(2):
                    bank = result_bank()
                    for c in range(DC):
                        ins = pe.matmul(bank[:, :], y1T[:, c, u * P:(u + 1) * P],
                                        w1T[:, c, h * BANK:(h + 1) * BANK], start=(c == 0), stop=(c == DC - 1))
                    ins.then_inc(result_ready, 1)

            def do_round(r, stage):
                more, before, late = stage + 1 < PAIRS, 1 <= stage <= PAIRS, stage >= 2
                front = 1 <= stage and more
                if front:
                    pe.wait_ge(xn_ready, (r + 2) * 2)
                    turn_pair(xn)
                    xn_landed = turned_so_far()
                if before:
                    pe.wait_ge(p_ready, r * 2)
                    turn_weights(1, 0)
                    landed_0 = turned_so_far()
                    turn_weights(1, 1)
                    landed_1 = turned_so_far()
                if front:
                    queries(0, xn_landed)
                if before:
                    bank = result_bank()
                    weighted(bank, 0, landed_0)
                if front:
                    queries(1, xn_landed)
                    pe.sem_inc(xn_turned, 1)
                    pe.wait_ge(q_high_ready, (r + 1) * DC + 1)
                if before:
                    turn_weights(1, 2)
                    landed_2 = turned_so_far()
                    weighted(bank, 1, landed_1)
                if front:
                    pe.wait_ge(q_high_ready, (r + 2) * DC)
                if before:
                    turn_weights(1, 3)
                    landed_3 = turned_so_far()
                    weighted(bank, 2, landed_2)
                    weighted(bank, 3, landed_3).then_inc(result_ready, 1)
                if front:
                    pe.wait_ge(q_low_ready, r + 2)
                    for c in range(SC):
                        scores(r * 2 + 2, 0, c)
                if stage < PAIRS:
                    pe.wait_ge(p_ready, r * 2 + 1)
                    turn_weights(0, 0)
                    landed_0 = turned_so_far()
                    turn_weights(0, 1)
                    landed_1 = turned_so_far()
                if more:
                    scores(r * 2 + 3, 1, 0)
                if stage < PAIRS:
                    bank = result_bank()
                    weighted(bank, 0, landed_0)
                    turn_weights(0, 2)
                    landed_2 = turned_so_far()
                    turn_weights(0, 3)
                    landed_3 = turned_so_far()
                    weighted(bank, 1, landed_1)
                    weighted(bank, 2, landed_2)
                    weighted(bank, 3, landed_3).then_inc(result_ready, 1)
                if stage == PAIRS:
                    pe.wait_ge(y1_ready, r * 2)
                    turn_pair(y1)
                    pe.wait_ge(turn_taken, turned_so_far())
                    up(0)
                    up(1)
                if late:
                    pe.wait_ge(y2_ready, (r - 2) * 2 + 1)
                    turn_y2(0, 0)
                    turn_y2(0, 1)
                if more:
                    scores(r * 2 + 3, 1, 1)
                if late:
                    pe.wait_ge(y2_ready, (r - 2) * 2 + 2)
                    turn_y2(1, 0)
                    turn_y2(1, 1)
                    for u in range(2):
                        bank = result_bank()
                        pe.wait_ge(turn_taken, turned_so_far() - 2 + 2 * u)
                        for b in range(FB):
                            ins = pe.matmul(bank[:, 0:D], y2T[:, b, u * P:(u + 1) * P], w2T[:, b, :],
                                            start=(b == 0), stop=(b == FB - 1))
                        ins.then_inc(result_ready, 1)
                if 1 <= stage < PAIRS:
                    pe.wait_ge(y1_ready, r * 2)
                    turn_pair(y1)
                    y1_landed = turned_so_far()
                if more:
                    scores(r * 2 + 3, 1, 2)
                if 1 <= stage < PAIRS:
                    pe.wait_ge(turn_taken, y1_landed)
                    up(0)
                if more:
                    scores(r * 2 + 3, 1, 3)
                if 1 <= stage < PAIRS:
                    up(1)

            rounds(pe, do_round, [turns, results])


_INS = ["x", "ctx_1024", "L0_xattn_Wq", "L0_xattn_bq", "L0_xattn_Wk", "L0_xattn_bk", "L0_xattn_Wv", "L0_xattn_bv",
        "L0_xattn_Wo", "L0_xattn_bo", "L0_ffn_w1", "L0_ffn_b1", "L0_ffn_w2", "L0_ffn_b2"]


def kernel(**inputs):
    from concourse import bacc
    from concourse.bass_utils import run_bass_kernel_spmd

    nc = bacc.Bacc("TRN2", target_bir_lowering=False, num_devices=1)
    arrays, args = {}, []
    for name in _INS:
        a = np.ascontiguousarray(inputs[name])
        arrays[f"in_{name}"] = a
        args.append(nc.dram_tensor(f"in_{name}", a.shape, mybir.dt.from_np(a.dtype), kind="ExternalInput").ap())
    args.append(nc.dram_tensor("out", (1, T, D), F32, kind="ExternalOutput").ap())
    build(nc, *args)
    r = run_bass_kernel_spmd(nc, [arrays], core_ids=[0])
    return r.results[0]["out"]
```
